# Optimizing a Trainium2 kernel written in Bass

```python
import numpy as np
import jax
import jax.numpy as jnp

def _softmax(x, axis=-1):
    return jax.nn.softmax(x, axis=axis)

def _gelu(x):
    return jax.nn.gelu(x, approximate=True)

def _silu(x):
    return jax.nn.silu(x)

def _sigmoid(x):
    return jax.nn.sigmoid(x)

def _layernorm(x, axis=-1, eps=1e-05):
    m = jnp.mean(x, axis=axis, keepdims=True)
    v = jnp.var(x, axis=axis, keepdims=True)
    return (x - m) / jnp.sqrt(v + eps)

def _scatter_add(tgt, idx, src, axis=0):
    return tgt.at[idx].add(src)

def _segment_sum(src, seg, n):
    return jax.ops.segment_sum(src, seg, n)
kernel_name = 'mk_gnn_preln_d1_gnn_r32_a49891'

def setup_inputs(seed: int=0):
    np.random.seed(seed)
    _w = jnp.asarray

    def _rec_inputs():
        import jax
        import jax.numpy as jnp
        _gk = jax.random.key(seed)
        x = -0.0006008 + 1.001 * jax.random.normal(jax.random.fold_in(_gk, 1), (3125, 256), jnp.float32)
        src = jax.random.randint(jax.random.fold_in(_gk, 2), (50000,), 0, 3125, jnp.int32)
        dst = jnp.minimum((3125 * jax.random.uniform(jax.random.fold_in(_gk, 3), (50000,)) ** 2.0).astype(jnp.int32), 99999)
        _o = jnp.argsort(dst, stable=True)
        src = src[_o]
        dst = dst[_o]
        return (x, src, dst)
    x, src, dst = _rec_inputs()

    def _L0_gnn_setup():
        import jax, jax.numpy as jnp
        import numpy as np
        N_NODES = 10000
        N_EDGES = 10000
        IN_CH = 256
        LATENT = 128
        OUT_CH = 256

        def _glorot(key, fan_in, fan_out):
            s = jnp.sqrt(2.0 / (fan_in + fan_out)).astype(jnp.float32)
            return jax.random.normal(key, (fan_in, fan_out), dtype=jnp.float32) * s

        def _sage_conv(x, src, dst, Wl, Wr, b):
            n = x.shape[0]
            agg = jax.ops.segment_sum(x[src], dst, num_segments=n)
            deg = jax.ops.segment_sum(jnp.ones_like(dst, dtype=x.dtype), dst, num_segments=n)
            mean = agg / jnp.maximum(deg, 1.0)[:, None]
            return mean @ Wl + x @ Wr + b
        key = jax.random.key(seed)
        ks = jax.random.split(key, 16)
        x = jax.random.normal(ks[0], (N_NODES, IN_CH), dtype=jnp.float32)
        edge_index = jax.random.randint(ks[1], (2, N_EDGES), 0, N_NODES, dtype=jnp.int64)
        dims = [(IN_CH, 2 * LATENT), (2 * LATENT, LATENT), (LATENT, 2 * LATENT), (2 * LATENT, OUT_CH)]
        params = {}
        for i, (fi, fo) in enumerate(dims, start=1):
            params[f'Wl{i}'] = _glorot(ks[2 + 3 * (i - 1)], fi, fo)
            params[f'Wr{i}'] = _glorot(ks[3 + 3 * (i - 1)], fi, fo)
            params[f'b{i}'] = jnp.zeros((fo,), dtype=jnp.float32)
        return {'x': x, 'edge_index': edge_index, **params}
    _L0_gnn_all = _L0_gnn_setup()
    _L0_gnn_in = {k: v for k, v in _L0_gnn_all.items() if k in ('Wl1', 'Wr1', 'b1', 'Wl2', 'Wr2', 'b2', 'Wl3', 'Wr3', 'b3', 'Wl4', 'Wr4', 'b4')}
    del _L0_gnn_all
    return {'x': x, 'src': src, 'dst': dst, 'L0_gnn_Wl1': _L0_gnn_in['Wl1'], 'L0_gnn_Wr1': _L0_gnn_in['Wr1'], 'L0_gnn_b1': _L0_gnn_in['b1'], 'L0_gnn_Wl2': _L0_gnn_in['Wl2'], 'L0_gnn_Wr2': _L0_gnn_in['Wr2'], 'L0_gnn_b2': _L0_gnn_in['b2'], 'L0_gnn_Wl3': _L0_gnn_in['Wl3'], 'L0_gnn_Wr3': _L0_gnn_in['Wr3'], 'L0_gnn_b3': _L0_gnn_in['b3'], 'L0_gnn_Wl4': _L0_gnn_in['Wl4'], 'L0_gnn_Wr4': _L0_gnn_in['Wr4'], 'L0_gnn_b4': _L0_gnn_in['b4']}

def reference(x, src, dst, L0_gnn_Wl1, L0_gnn_Wr1, L0_gnn_b1, L0_gnn_Wl2, L0_gnn_Wr2, L0_gnn_b2, L0_gnn_Wl3, L0_gnn_Wr3, L0_gnn_b3, L0_gnn_Wl4, L0_gnn_Wr4, L0_gnn_b4):
    import jax
    import jax.numpy as jnp

    def _L0_gnn_ref(x, edge_index, Wl1, Wr1, b1, Wl2, Wr2, b2, Wl3, Wr3, b3, Wl4, Wr4, b4):
        import jax, jax.numpy as jnp
        import numpy as np
        N_NODES = 10000
        N_EDGES = 10000
        IN_CH = 256
        LATENT = 128
        OUT_CH = 256

        def _glorot(key, fan_in, fan_out):
            s = jnp.sqrt(2.0 / (fan_in + fan_out)).astype(jnp.float32)
            return jax.random.normal(key, (fan_in, fan_out), dtype=jnp.float32) * s

        def _sage_conv(x, src, dst, Wl, Wr, b):
            n = x.shape[0]
            agg = jax.ops.segment_sum(x[src], dst, num_segments=n)
            deg = jax.ops.segment_sum(jnp.ones_like(dst, dtype=x.dtype), dst, num_segments=n)
            mean = agg / jnp.maximum(deg, 1.0)[:, None]
            return mean @ Wl + x @ Wr + b
        src, dst = (edge_index[0], edge_index[1])
        h = jax.nn.relu(_sage_conv(x, src, dst, Wl1, Wr1, b1))
        h = jax.nn.relu(_sage_conv(h, src, dst, Wl2, Wr2, b2))
        h = jax.nn.relu(_sage_conv(h, src, dst, Wl3, Wr3, b3))
        return _sage_conv(h, src, dst, Wl4, Wr4, b4)
    edge_index = jnp.stack([src, dst])
    h = jnp.maximum(_layernorm(x, axis=-1), 0.0)
    x = x + _L0_gnn_ref(h, edge_index, L0_gnn_Wl1, L0_gnn_Wr1, L0_gnn_b1, L0_gnn_Wl2, L0_gnn_Wr2, L0_gnn_b2, L0_gnn_Wl3, L0_gnn_Wr3, L0_gnn_b3, L0_gnn_Wl4, L0_gnn_Wr4, L0_gnn_b4)
    return x

_drawn_inputs = setup_inputs


def setup_inputs(seed=0):
    import zlib

    import numpy as np

    out = dict(_drawn_inputs(seed))
    spreads = {'L0_gnn_b1': (0.0, 0.1),
     'L0_gnn_b2': (0.0, 0.1),
     'L0_gnn_b3': (0.0, 0.1),
     'L0_gnn_b4': (0.0, 0.1)}
    factors = {}
    for name, (base, spread) in spreads.items():
        noise = np.random.default_rng([zlib.crc32(name.encode()), seed]).standard_normal(out[name].shape)
        drawn = base * np.exp(spread * noise) if base else spread * noise
        out[name] = jnp.asarray(drawn.astype(out[name].dtype))
    for name, factor in factors.items():
        out[name] = (out[name] * factor).astype(out[name].dtype)
    return out
```

```python
import concourse.bass as bass
from concourse import mybir
from contextlib import ExitStack, contextmanager


class Order:

    def __init__(self, engine, semaphore):
        self.engine, self.semaphore, self.count, self.before = engine, semaphore, 0, 0

    def after(self, instruction):
        instruction.then_inc(self.semaphore, 1)
        self.count += 1
        self.engine.wait_ge(self.semaphore, self.before + self.count)

    @contextmanager
    def rounds(self, done_rounds, per_round, n_rounds):
        start = self.count
        self.before, self.count = done_rounds * per_round + start, 0
        yield
        assert self.count == per_round, (self.count, per_round)
        self.before, self.count = 0, start + per_round * n_rounds


def sage_stack_kernel(nc, x, src, dst, Wl1, Wr1, b1, Wl2, Wr2, b2, Wl3, Wr3, b3, Wl4, Wr4, b4, out):
    f32, f16, i32 = mybir.dt.float32, mybir.dt.float16, mybir.dt.int32
    ALU, ACT, AX = mybir.AluOpType, mybir.ActivationFunctionType, mybir.AxisListType

    P = 128
    N, D = x.shape
    E = src.shape[0]
    F2 = Wl2.shape[1]
    NT = -(-N // P)
    TAIL = N - (NT - 1) * P
    TPC = 4
    CH = TPC * P
    NFULL = (NT - 1) // TPC
    NCH = NFULL + 1
    assert NFULL * TPC == NT - 1 and 0 < TAIL <= P
    ET = -(-E // P)
    EG = -(-ET // P)
    WIN = 16
    NWIN = -(-N // WIN)
    WPC = CH // WIN
    WTAIL = NWIN - NFULL * WPC
    KEYS = WIN * NT
    NPAD = NWIN * WIN
    PAD_DST = NPAD - 1
    assert PAD_DST >= N
    WP = NWIN // 2
    assert WP * 2 == NWIN and WP <= P
    RING = 4
    STEP_MASK = (1 << (NWIN * ET).bit_length()) - 1
    H0_SCALE = 2048.0
    FP16_ROOM = 32768.0
    EPS = 1e-5
    FAR = 1024.0

    ctx = ExitStack()
    with ctx:
        def sb(name, shape, dt):
            return ctx.enter_context(nc.sbuf_tensor(name, shape, dt))

        def pb(name, shape, dt):
            return ctx.enter_context(nc.psum_tensor(name, shape, dt))

        def sem(name):
            return ctx.enter_context(nc.semaphore(name))

        counts = sb("counts", [P, NT, NPAD], f16)
        H = sb("H", [P, NT, 2, D], f16)
        Hn = H[:, :, :, :].rearrange("p t h f -> p (t h f)")[:, 0:NT * 2 * F2].rearrange(
            "p (t h f) -> p t h f", t=NT, h=2)
        hot_src = sb("hot_src", [P, RING, P], f16)
        hot_key = sb("hot_key", [P, RING, KEYS], f16)
        src_numbers = sb("src_numbers", [P, P], f16)
        key_numbers = sb("key_numbers", [P, NT, WIN], f16)
        edge_src = sb("edge_src", [P, EG * P], f32)
        edge_key = sb("edge_key", [P, EG * P], f32)
        win_key = sb("win_key", [P, NWIN], f32)
        plan = sb("plan", [1, NWIN, 4], i32)
        W14 = sb("W14", [P, 2, 2, D], f32)
        W2 = sb("W2", [P, 2, 2, F2], f32)
        W3 = sb("W3", [P, 2, D], f32)
        aggT = sb("aggT", [P, 2, CH], f32)
        selfT = sb("selfT", [P, 2, CH], f32)
        newT = sb("newT", [P, 2, CH], f32)
        partsT = sb("partsT", [P, 2, CH], f16)
        newH = sb("newH", [P, TPC, 2, D], f16)
        rdeg = sb("rdeg", [P, CH], f32)
        ident16 = sb("ident16", [P, P], f16)
        ident32 = sb("ident32", [P, P], f32)
        ones16 = sb("ones16", [P, P], f16)
        bT = sb("bT", [P, 5], f32)
        scale = sb("scale", [P, 3], f32)
        unscale = sb("unscale", [P, 4], f32)
        stats = sb("stats", [P, TPC, 6], f32)
        moments = sb("moments", [P, TPC, 2], f32)
        rstd = sb("rstd", [P, TPC], f32)
        shift = sb("shift", [P, TPC], f32)
        eps = sb("eps", [P, 1], f32)
        b4rows = sb("b4rows", [P, D], f32)

        spare = counts[:, :, :].rearrange("p t n -> p (t n)").bitcast(f32)
        taken = [0]

        def scratch(*shape):
            size = 1
            for s in shape:
                size *= s
            at = spare[:, taken[0]:taken[0] + size]
            taken[0] += size
            if len(shape) == 2:
                at = at.rearrange("p (a b) -> p a b", a=shape[0])
            if len(shape) == 3:
                at = at.rearrange("p (a b c) -> p a b c", a=shape[0], b=shape[1])
            return at

        src_rows = scratch(EG, P).bitcast(i32)
        dst_rows = scratch(EG, P).bitcast(i32)
        tile_rows = scratch(EG, P).bitcast(i32)
        within_rows = scratch(EG, P).bitcast(i32)
        dst_f = scratch(EG, P)
        tile_f = scratch(EG, P)
        within_f = scratch(EG, P)
        key_f = scratch(EG, P)
        span = scratch(2, EG)
        spans = scratch(2, EG * P)
        tile_up = scratch(EG * P)
        tile_down = scratch(EG * P)
        win_first = scratch(2)
        win_last = scratch(2)
        meets = scratch(2, EG * P)
        meets_b = scratch(2, EG * P)
        picked = scratch(2, EG * P)
        lo_far = scratch(2)
        lo_hi = scratch(2, 2)
        rows = scratch(2, 2, WP)
        lengths = scratch(NWIN)
        zeros_row = scratch(NWIN)
        ends = scratch(NWIN)
        planf = scratch(NWIN, 4)
        ones32 = scratch(P)
        wsq = scratch(2, 2, D)
        norms = scratch(6, D)
        bias_rows = scratch(3, D)
        bound = scratch(D)
        bound_b = scratch(D)
        sq_row = scratch(D)
        rownorm = scratch(4)
        tops = scratch(3)

        window_ps = pb("window_ps", [P, 2, 512], f32)
        degree_ps = pb("degree_ps", [P, 512], f32)
        agg_ps = pb("agg_ps", [P, 2, 512], f32)
        lin_ps = pb("lin_ps", [P, 2, 512], f32)
        turn_ps = pb("turn_ps", [P, 2 * TPC, P], f16)

        span_d = nc.dram_tensor("span_d", [2, EG, P], f32, kind="Internal").ap()
        rdeg_d = nc.dram_tensor("rdeg_d", [1, NCH * CH], f32, kind="Internal").ap()
        hT_d = [nc.dram_tensor(f"hT{i}_d", [P, 2, NCH * CH], f32, kind="Internal").ap() for i in range(4)]
        H_d = [None] + [nc.dram_tensor(f"H{i}_d", [P, NT, 2 * w], f16, kind="Internal").ap()
                        for i, w in ((1, F2), (2, F2), (3, D))]

        dve_order = sem("dve_order")
        act_order = sem("act_order")
        pool_order = sem("pool_order")
        pads_set = sem("pads_set")
        consts_made = sem("consts_made")
        edges_loaded = sem("edges_loaded")
        weights_loaded = sem("weights_loaded")
        w4_loaded = sem("w4_loaded")
        spans_found = sem("spans_found")
        spans_stored = sem("spans_stored")
        spans_loaded = sem("spans_loaded")
        edge_rows_ready = sem("edge_rows_ready")
        edges_turned = sem("edges_turned")
        ranges_found = sem("ranges_found")
        ranges_turned = sem("ranges_turned")
        plan_made = sem("plan_made")
        squares_made = sem("squares_made")
        squares_summed = sem("squares_summed")
        norms_made = sem("norms_made")
        scales_made = sem("scales_made")
        x_loaded = [sem("x_loaded0"), sem("x_loaded1")]
        tail_cleared = sem("tail_cleared")
        moments_made = sem("moments_made")
        root_made = sem("root_made")
        shift_made = sem("shift_made")
        h0_made = sem("h0_made")
        h0_high = sem("h0_high")
        h0_low = sem("h0_low")
        h0_turned = sem("h0_turned")
        h0T_copied = sem("h0T_copied")
        hot_made = sem("hot_made")
        hot_free = sem("hot_free")
        window_counted = sem("window_counted")
        window_stored = sem("window_stored")
        rdeg_made = sem("rdeg_made")
        rdeg_stored = sem("rdeg_stored")
        hT_stored = [sem(f"hT{i}_stored") for i in range(4)]
        L = range(5)
        self_loaded = [sem(f"self_loaded_{i}") for i in L]
        rdeg_loaded = [sem(f"rdeg_loaded_{i}") for i in L]
        agg_done = [sem(f"agg_done_{i}") for i in L]
        agg_scaled = [sem(f"agg_scaled_{i}") for i in L]
        lin_done = [sem(f"lin_done_{i}") for i in L]
        relu_done = [sem(f"relu_done_{i}") for i in L]
        high_done = [sem(f"high_done_{i}") for i in L]
        low_done = [sem(f"low_done_{i}") for i in L]
        turned = [sem(f"turned_{i}") for i in L]
        turn_copied = [sem(f"turn_copied_{i}") for i in L]
        H_stored = [sem(f"H_stored_{i}") for i in L]
        narrow_done = sem("narrow_done")
        summed = sem("summed")
        H_loaded = [sem(f"H_loaded_{i}") for i in range(NCH)]
        x4_loaded = sem("x4_loaded")
        b4_loaded = sem("b4_loaded")
        x4_biased = sem("x4_biased")
        out_made = sem("out_made")
        out_stored = sem("out_stored")

        AGG = [0, 2, 1, 1, 2]
        SELF = [0, 2, 2, 1, 2]
        NEW = [0, 2, 1, 2, 2]
        TURNS = [0, 1, 1, 2, 0]
        LIN = [0, 2, 1, 2, 2]
        FULL = (CH, TPC)
        LAST = (TAIL, 1)

        NW = 12
        CONSTS = 13
        x4 = newH[:, :, :, :].rearrange("p t h f -> p (t h f)").bitcast(f32).rearrange("p (t f) -> p t f", t=TPC)

        def newH_flat(width):
            return newH[:, :, :, :].rearrange("p t h f -> p (t h f)")[:, 0:TPC * width].rearrange(
                "p (t w) -> p t w", t=TPC)

        def size_of(c):
            return LAST if isinstance(c, int) and c == NFULL else FULL

        def chunk_cols(c, n):
            return bass.ds(c * CH, n)

        block = ctx.enter_context(nc.Block())

        @block.sync
        def _(sp):
            sp.wait_ge(pads_set, 2)
            full = E // P // P * P
            more = E // P - full
            for rows_, edges in ((src_rows, src), (dst_rows, dst)):
                sp.dma_start(rows_[:, 0:full // P, :],
                             edges[0:full * P].rearrange("(g p e) -> p g e", p=P, e=P)).then_inc(edges_loaded, 16)
                sp.dma_start(rows_[0:more, full // P, :],
                             edges[full * P:(full + more) * P].rearrange("(p e) -> p e", e=P)
                             ).then_inc(edges_loaded, 16)
                rest = E - (full + more) * P
                sp.dma_start(rows_[more:more + 1, full // P, 0:rest],
                             edges[(full + more) * P:E].rearrange("(p e) -> p e", p=1)).then_inc(edges_loaded, 16)

            def load_x(c, slot):
                n, t = size_of(c)
                buf = (aggT if slot == 0 else selfT)[:, :, :].rearrange("p a b -> p (a b)").rearrange(
                    "p (t f) -> p t f", t=TPC)
                if n == CH:
                    sp.dma_start(buf, x_chunk(c)).then_inc(x_loaded[slot], 16)
                else:
                    sp.dma_start(buf[0:n, 0, :], x[c * CH:N, :]).then_inc(x_loaded[slot], 16)

            def x_chunk(c):
                return x[chunk_cols(c, CH), :].rearrange("(t p) f -> p t f", p=P)

            def store_h0T(c):
                n, t = size_of(c)
                sp.wait_ge(h0T_copied, 2 * (c + 1))
                sp.dma_start(hT_d[0][:, :, chunk_cols(c, n)], newT[:, :, 0:n]).then_inc(hT_stored[0], 16)

            load_x(0, 0)
            load_x(1, 1)
            nw = 0

            def small(dst_ap, src_ap, scattered=False):
                nonlocal nw
                nw += 1
                sp.dma_start(dst_ap, src_ap, allow_slow_non_contiguous=scattered).then_inc(weights_loaded, 16)

            for i, w in enumerate((Wl1, Wr1)):
                small(W14[:, i, :, :], w.rearrange("(k p) n -> p k n", p=P))
            for i, w in enumerate((Wl2, Wr2)):
                small(W2[:, i, :, :], w.rearrange("(k p) n -> p k n", p=P))
            for i, w in enumerate((Wl3, Wr3)):
                small(W3[:, i, :], w)
            small(bT[:, 0:2], b1.rearrange("(k p) -> p k", p=P), True)
            small(bT[:, 2:3], b2.rearrange("(k p) -> p k", p=P), True)
            small(bT[:, 3:5], b3.rearrange("(k p) -> p k", p=P), True)
            for i, b in enumerate((b1, b2, b3)):
                small(bias_rows[:, i, 0:b.shape[0]],
                      b.rearrange("(o n) -> o n", o=1).broadcast_to([P, b.shape[0]]))
            assert nw == NW

            sp.wait_ge(spans_found, 1)
            sp.dma_start(span_d.rearrange("a g p -> p a g"), span[:, :, :], allow_slow_non_contiguous=True
                         ).then_inc(spans_stored, 16)
            sp.wait_ge(spans_stored, 16)
            sp.dma_start(spans[:, :, :], span_d.rearrange("a g p -> a (g p)").unsqueeze(0).broadcast_to(
                [P, 2, EG * P])).then_inc(spans_loaded, 16)

            with sp.Fori(0, NFULL // 2 - 1) as i:
                store_h0T(2 * i)
                sp.wait_ge(h0_low, 2 * i + 1)
                load_x(2 * i + 2, 0)
                store_h0T(2 * i + 1)
                sp.wait_ge(h0_low, 2 * i + 2)
                load_x(2 * i + 3, 1)
            store_h0T(NFULL - 2)
            sp.wait_ge(h0_low, NFULL - 1)
            sp.wait_ge(tail_cleared, 1)
            load_x(NFULL, 0)
            store_h0T(NFULL - 1)
            store_h0T(NFULL)

            for l in (1, 2, 3, 4):
                sp.wait_ge(hT_stored[l - 1], 16 * NCH)

                def load_self(c):
                    n, t = size_of(c)
                    sp.dma_start(selfT[:, 0:SELF[l], 0:n], hT_d[l - 1][:, 0:SELF[l], chunk_cols(c, n)]
                                 ).then_inc(self_loaded[l], 16)

                def load_rdeg(c):
                    n, t = size_of(c)
                    sp.dma_start(rdeg[:, 0:n], rdeg_d[0:1, chunk_cols(c, n)].broadcast_to([P, n])
                                 ).then_inc(rdeg_loaded[l], 16)

                def store_rdeg(c):
                    n, t = size_of(c)
                    sp.wait_ge(rdeg_made, c + 1)
                    sp.dma_start(rdeg_d[0:1, chunk_cols(c, n)], rdeg[0:1, 0:n]).then_inc(rdeg_stored, 16)

                def stores(c):
                    n, t = size_of(c)
                    if l < 4:
                        sp.wait_ge(relu_done[l], NEW[l] * (c + 1))
                        sp.dma_start(hT_d[l][:, 0:NEW[l], chunk_cols(c, n)], newT[:, 0:NEW[l], 0:n]
                                     ).then_inc(hT_stored[l], 16)
                        sp.wait_ge(turn_copied[l], TURNS[l] * (c + 1))
                        w = 2 * F2 * TURNS[l]
                        sp.dma_start(H_d[l][:, bass.ds(c * TPC, t), :], newH_flat(w)[:, 0:t, :]
                                     ).then_inc(H_stored[l], 16)
                    else:
                        sp.wait_ge(out_made, 2 * (c + 1) if n == CH else 2 * NFULL + 1)
                        o = newT[:, :, :].rearrange("p a b -> p (a b)").rearrange("p (t f) -> p t f", t=TPC)
                        if n == CH:
                            sp.dma_start(out[chunk_cols(c, CH), :].rearrange("(t p) f -> p t f", p=P), o
                                         ).then_inc(out_stored, 16)
                        else:
                            sp.dma_start(out[c * CH:N, :], o[0:n, 0, :]).then_inc(out_stored, 16)

                def load_x4(c):
                    n, t = size_of(c)
                    if n == CH:
                        sp.dma_start(x4[:, :, :], x_chunk(c)).then_inc(x4_loaded, 16)
                    else:
                        sp.dma_start(x4[0:n, 0, :], x[c * CH:N, :]).then_inc(x4_loaded, 16)

                def step(c):
                    if l == 1:
                        store_rdeg(c)
                    sp.wait_ge(lin_done[l], LIN[l] * c)
                    load_self(c)
                    if l > 1:
                        sp.wait_ge(agg_scaled[l], AGG[l] * (c + 1))
                        if not (isinstance(c, int) and c == NFULL):
                            load_rdeg(c + 1 if isinstance(c, int) else c + 1)
                    stores(c - 1)
                    if l == 4:
                        sp.wait_ge(out_made, 2 * c)
                        load_x4(c)

                load_self(0)
                if l == 1:
                    store_rdeg(0)
                else:
                    if l == 2:
                        sp.wait_ge(rdeg_stored, 16 * NCH)
                    load_rdeg(0)
                    sp.wait_ge(agg_scaled[l], AGG[l])
                    load_rdeg(1)
                if l == 2:
                    sp.wait_ge(lin_done[1], LIN[1] * NCH)
                    sp.dma_start(W14[:, 0, :, :], Wl4.rearrange("(k p) n -> p k n", p=P)).then_inc(w4_loaded, 16)
                    sp.dma_start(W14[:, 1, :, :], Wr4.rearrange("(k p) n -> p k n", p=P)).then_inc(w4_loaded, 16)
                    sp.dma_start(b4rows[:, :], b4.rearrange("(o n) -> o n", o=1).broadcast_to([P, D])
                                 ).then_inc(b4_loaded, 16)
                if l == 4:
                    load_x4(0)
                with sp.Fori(1, NFULL - 1) as c:
                    step(c)
                if l == 1:
                    store_rdeg(NFULL - 1)
                sp.wait_ge(lin_done[l], LIN[l] * (NFULL - 1))
                load_self(NFULL - 1)
                if l > 1:
                    sp.wait_ge(agg_scaled[l], AGG[l] * NFULL)
                    load_rdeg(NFULL)
                stores(NFULL - 2)
                if l == 4:
                    sp.wait_ge(out_made, 2 * (NFULL - 1))
                    load_x4(NFULL - 1)
                step(NFULL)
                if l < 4:
                    sp.wait_ge(agg_done[l], AGG[l] * NCH)
                    sp.wait_ge(H_stored[l], 16 * NFULL)
                    H_to = (H[:, :, :, :] if TURNS[l] == 2 else Hn).rearrange("p t h f -> p t (h f)")
                    for c in range(NFULL):
                        sp.dma_start(H_to[:, c * TPC:(c + 1) * TPC, :], H_d[l][:, c * TPC:(c + 1) * TPC, :]
                                     ).then_inc(H_loaded[c], 16)
                stores(NFULL)
                if l < 4:
                    sp.wait_ge(H_stored[l], 16 * NCH)
                    sp.dma_start(H_to[:, NT - 1:NT, :], H_d[l][:, NT - 1:NT, :]).then_inc(H_loaded[NFULL], 16)
            sp.wait_ge(out_stored, 16 * NCH)

        @block.gpsimd
        def _(pool):
            order = Order(pool, pool_order)
            nc.gpsimd.memset(src_rows[:, EG - 1, :], 0).then_inc(pads_set, 1)
            nc.gpsimd.memset(dst_rows[:, EG - 1, :], PAD_DST).then_inc(pads_set, 1)
            order.after(nc.gpsimd.memset(ident32[:, :], 0.0))
            order.after(nc.gpsimd.affine_select(out=ident32[:, :], in_=ident32[:, :], compare_op=ALU.not_equal,
                                                fill=1.0, base=0, pattern=[[-1, P]], channel_multiplier=1))
            nc.gpsimd.tensor_copy(ident16[:, :], ident32[:, :]).then_inc(consts_made, 1)
            nc.gpsimd.memset(ones16[:, :], 1.0).then_inc(consts_made, 1)
            nc.gpsimd.memset(ones32, 1.0).then_inc(consts_made, 1)
            nc.gpsimd.memset(zeros_row, 0.0).then_inc(consts_made, 1)
            nc.gpsimd.memset(eps[:, :], EPS).then_inc(consts_made, 1)
            nc.gpsimd.memset(unscale[:, 0:1], 1.0 / H0_SCALE).then_inc(consts_made, 1)

            def numbers(ap, pattern, base=0, rows=0):
                nc.gpsimd.iota(ap, pattern=pattern, base=base, channel_multiplier=rows,
                               allow_small_or_imprecise_dtypes=True).then_inc(consts_made, 1)

            numbers(src_numbers[:, :], [[1, P]])
            numbers(key_numbers[:, :, :], [[1, NT], [NT, WIN]])
            numbers(win_key[:, :], [[-KEYS, NWIN]])
            numbers(tile_up, [[1, EG * P]], base=1)
            numbers(tile_down, [[-1, EG * P]], base=int(FAR))
            numbers(win_first, [[WIN * WP, 2]], rows=WIN)
            numbers(win_last, [[WIN * WP, 2]], base=WIN - 1, rows=WIN)
            assert CONSTS == 13
            pool.wait_ge(b4_loaded, 16)

            def bias_x(c):
                n, t = size_of(c)
                pool.wait_ge(x4_loaded, 16 * (c + 1))
                for i in range(t):
                    q = P if n == CH else n
                    nc.gpsimd.tensor_tensor(x4[0:q, i, :], x4[0:q, i, :], b4rows[0:q, :], ALU.add
                                            ).then_inc(x4_biased, 1)

            with pool.Fori(0, NFULL) as c:
                bias_x(c)
            bias_x(NFULL)

        def window_steps(eng, w, regs):
            eng.load(regs, plan[0:1, w if isinstance(w, int) else bass.ds(w, 1), 0:3])
            first = eng.snap(regs[0], min_val=0, max_val=ET - 1)
            steps = eng.snap(regs[1], min_val=1, max_val=ET)
            before = eng.snap(regs[2], min_val=0, max_val=NWIN * ET) & STEP_MASK
            return first, steps, before

        @block.vector
        def _(dve):
            order = Order(dve, dve_order)
            v = nc.vector
            dve.wait_ge(consts_made, CONSTS)
            dve.wait_ge(edges_loaded, 16 * 6)
            order.after(v.tensor_copy(dst_f, dst_rows))
            order.after(v.tensor_reduce(out=span[:, 0, :], in_=dst_f, axis=AX.X, op=ALU.min))
            v.tensor_reduce(out=span[:, 1, :], in_=dst_f, axis=AX.X, op=ALU.max).then_inc(spans_found, 1)
            order.after(v.tensor_single_scalar(tile_rows, src_rows, 7, ALU.logical_shift_right))
            order.after(v.tensor_single_scalar(within_rows, src_rows, P - 1, ALU.bitwise_and))
            order.after(v.tensor_copy(tile_f, tile_rows))
            v.tensor_copy(within_f, within_rows).then_inc(edge_rows_ready, 1)
            v.scalar_tensor_tensor(out=key_f, in0=dst_f, scalar=float(NT), in1=tile_f, op0=ALU.mult,
                                   op1=ALU.add).then_inc(edge_rows_ready, 1)
            dve.wait_ge(weights_loaded, 16 * NW)
            v.tensor_tensor(wsq[:, :, :, :], W14[:, :, :, :], W14[:, :, :, :], ALU.mult).then_inc(squares_made, 1)
            dve.wait_ge(edges_turned, 2)
            order.after(v.tensor_copy(edge_key[:, :], window_ps[:, 0, 0:EG * P]))
            order.after(v.tensor_copy(edge_src[:, :], window_ps[:, 1, 0:EG * P]))
            dve.wait_ge(spans_loaded, 16)
            for h in range(2):
                order.after(v.tensor_scalar(meets[0:WP, h, :], spans[0:WP, 0, :], win_last[0:WP, h:h + 1], None,
                                            ALU.is_le))
                order.after(v.scalar_tensor_tensor(out=meets_b[0:WP, h, :], in0=spans[0:WP, 1, :],
                                                   scalar=win_first[0:WP, h:h + 1], in1=meets[0:WP, h, :],
                                                   op0=ALU.is_ge, op1=ALU.mult))
                order.after(v.tensor_tensor(picked[0:WP, h, :], meets_b[0:WP, h, :], tile_up[0:WP, :], ALU.mult))
                order.after(v.tensor_reduce(out=lo_hi[0:WP, 1, h:h + 1], in_=picked[0:WP, h, :], axis=AX.X,
                                            op=ALU.max))
                order.after(v.tensor_tensor(picked[0:WP, h, :], meets_b[0:WP, h, :], tile_down[0:WP, :], ALU.mult))
                order.after(v.tensor_reduce(out=lo_far[0:WP, h:h + 1], in_=picked[0:WP, h, :], axis=AX.X,
                                            op=ALU.max))
            order.after(v.tensor_scalar(lo_hi[0:WP, 0, :], lo_far[0:WP, :], -1.0, FAR, ALU.mult, ALU.add))
            order.after(v.tensor_scalar(lo_hi[0:WP, 0, :], lo_hi[0:WP, 0, :], float(ET - 1), None, ALU.min))
            order.after(v.tensor_scalar(lo_far[0:WP, :], lo_hi[0:WP, 0, :], 1.0, None, ALU.add))
            order.after(v.tensor_scalar(lo_hi[0:WP, 1, :], lo_hi[0:WP, 1, :], float(ET), None, ALU.min))
            v.tensor_tensor(lo_hi[0:WP, 1, :], lo_hi[0:WP, 1, :], lo_far[0:WP, :], ALU.max).then_inc(ranges_found, 1)
            dve.wait_ge(ranges_turned, 1)
            for a in range(2):
                order.after(v.tensor_copy(rows[0:1, a, :, :], degree_ps[0:1, 256 * a:256 * a + 2 * WP].rearrange(
                    "p (h w) -> p h w", h=2)))
            lo_row = rows[0:1, 0, :, :].rearrange("p h w -> p (h w)")
            hi_row = rows[0:1, 1, :, :].rearrange("p h w -> p (h w)")
            order.after(v.tensor_tensor(lengths[0:1, :], hi_row, lo_row, ALU.subtract))
            order.after(v.tensor_tensor_scan(ends[0:1, :], zeros_row[0:1, :], lengths[0:1, :], 0.0, ALU.add, ALU.add))
            order.after(v.tensor_tensor(planf[0:1, :, 2], ends[0:1, :], lengths[0:1, :], ALU.subtract))
            order.after(v.tensor_copy(planf[0:1, :, 0], lo_row))
            order.after(v.tensor_copy(planf[0:1, :, 1], lengths[0:1, :]))
            v.tensor_copy(plan[0:1, :, 0:3], planf[0:1, :, 0:3]).then_inc(plan_made, 1)

            dve.wait_ge(squares_summed, 1)
            dve.wait_ge(norms_made, 1)
            v.tensor_tensor(wsq[:, :, :, 0:F2], W2[:, :, :, :], W2[:, :, :, :], ALU.mult).then_inc(squares_made, 1)
            dve.wait_ge(norms_made, 2)
            v.tensor_tensor(wsq[:, 0, :, :], W3[:, :, :], W3[:, :, :], ALU.mult).then_inc(squares_made, 1)
            dve.wait_ge(norms_made, 3)

            def row_norm(into, row):
                order.after(v.tensor_tensor(sq_row[:, 0:row.shape[-1]], row, row, ALU.mult))
                v.tensor_reduce(out=into, in_=sq_row[:, 0:row.shape[-1]], axis=AX.X, op=ALU.add
                                ).then_inc(norms_made, 1)

            root_d = float(D) ** 0.5
            order.after(v.tensor_tensor(bound, norms[:, 0, :], norms[:, 1, :], ALU.add))
            order.after(v.tensor_single_scalar(bound, bound, root_d, ALU.mult))
            order.after(v.scalar_tensor_tensor(out=bound_b, in0=bias_rows[:, 0, :], scalar=-1.0, in1=bias_rows[:, 0, :],
                                               op0=ALU.mult, op1=ALU.max))
            order.after(v.tensor_tensor(bound, bound, bound_b, ALU.add))
            row_norm(rownorm[:, 0:1], bound)
            dve.wait_ge(norms_made, 5)
            b2_ = bound[:, 0:F2]
            order.after(v.tensor_scalar(b2_, norms[:, 2, 0:F2], rownorm[:, 1:2], None, ALU.mult))
            order.after(v.tensor_reduce(out=tops[:, 0:1], in_=b2_, axis=AX.X, op=ALU.max))
            order.after(v.scalar_tensor_tensor(out=b2_, in0=norms[:, 3, 0:F2], scalar=rownorm[:, 1:2], in1=b2_,
                                               op0=ALU.mult, op1=ALU.add))
            order.after(v.scalar_tensor_tensor(out=bound_b[:, 0:F2], in0=bias_rows[:, 1, 0:F2], scalar=-1.0, in1=bias_rows[:, 1, 0:F2],
                                               op0=ALU.mult, op1=ALU.max))
            order.after(v.tensor_tensor(b2_, b2_, bound_b[:, 0:F2], ALU.add))
            order.after(v.tensor_reduce(out=tops[:, 1:2], in_=b2_, axis=AX.X, op=ALU.max))
            row_norm(rownorm[:, 2:3], b2_)
            dve.wait_ge(norms_made, 7)
            order.after(v.tensor_tensor(bound, norms[:, 4, :], norms[:, 5, :], ALU.add))
            order.after(v.tensor_scalar(bound, bound, rownorm[:, 3:4], None, ALU.mult))
            order.after(v.scalar_tensor_tensor(out=bound_b, in0=bias_rows[:, 2, :], scalar=-1.0, in1=bias_rows[:, 2, :],
                                               op0=ALU.mult, op1=ALU.max))
            order.after(v.tensor_tensor(bound, bound, bound_b, ALU.add))
            order.after(v.tensor_reduce(out=tops[:, 2:3], in_=bound, axis=AX.X, op=ALU.max))
            order.after(v.tensor_scalar(tops, tops, 1e-30, 1.0 / FP16_ROOM, ALU.max, ALU.mult))
            order.after(v.reciprocal(tops, tops))
            order.after(v.tensor_single_scalar(scale[:, :].bitcast(i32), tops.bitcast(i32), 0x7F800000,
                                               ALU.bitwise_and))
            v.reciprocal(unscale[:, 1:4], scale[:, :]).then_inc(scales_made, 1)

            def xbuf(slot):
                return (aggT if slot == 0 else selfT)[:, :, :].rearrange("p a b -> p (a b)").rearrange(
                    "p (t f) -> p t f", t=TPC)

            def h0_chunk(c, slot, uses):
                n, t = size_of(c)
                dve.wait_ge(x_loaded[slot], 16 * uses)
                for i in range(t):
                    v.bn_stats(stats[:, i, :], xbuf(slot)[:, i, :])
                dve.drain()
                for i in range(t):
                    v.bn_aggr(moments[:, i, :], stats[:, i, :]).then_inc(moments_made, 1)
                dve.wait_ge(root_made, c + 1)
                order.after(v.reciprocal(rstd[:, 0:t], rstd[:, 0:t]))
                v.scalar_tensor_tensor(out=shift[:, 0:t], in0=moments[:, 0:t, 0], scalar=-1.0, in1=rstd[:, 0:t],
                                       op0=ALU.mult, op1=ALU.mult).then_inc(shift_made, 1)
                dve.wait_ge(h0_high, c + 1)
                v.scalar_tensor_tensor(out=H[:, bass.ds(c * TPC, t), 1, :], in0=xbuf(slot)[:, 0:t, :],
                                       scalar=H0_SCALE, in1=H[:, bass.ds(c * TPC, t), 0, :], op0=ALU.mult,
                                       op1=ALU.subtract).then_inc(h0_low, 1)
                dve.wait_ge(h0_turned, 2 * c + 1)
                dve.wait_ge(hT_stored[0], 16 * c)
                nn = CH if n == CH else P
                v.tensor_copy(newT[:, 0, 0:nn], lin_ps[:, 0, 0:nn]).then_inc(h0T_copied, 1)

            per = 1
            with dve.Fori(0, NFULL // 2) as i:
                with order.rounds(i, 2 * per, NFULL // 2):
                    h0_chunk(2 * i, 0, i + 1)
                    h0_chunk(2 * i + 1, 1, i + 1)
            dve.wait_ge(h0T_copied, 2 * (NFULL - 1))
            v.memset(xbuf(0)[:, 0, :], 0.0).then_inc(tail_cleared, 1)
            h0_chunk(NFULL, 0, NFULL // 2 + 1)

            regs = [dve.alloc_register(f"dve_plan{i}") for i in range(3)]

            def window(w):
                first, steps, before = window_steps(dve, w, regs)
                with dve.Fori(0, steps) as i:
                    tile, step = (first + i).with_bounds(min_val=0, max_val=ET - 1), before + i
                    slot = step & (RING - 1)
                    dve.wait_ge(hot_free, step + 1)
                    v.tensor_scalar(hot_src[:, bass.ds(slot, 1), :], src_numbers[:, :].unsqueeze(1),
                                    edge_src[:, bass.ds(tile, 1)], None, ALU.is_equal).then_inc(hot_made, 1)
                    v.tensor_scalar(hot_key[:, bass.ds(slot, 1), :], key_numbers[:, :, :].rearrange(
                        "p t w -> p (t w)").unsqueeze(1), edge_key[:, bass.ds(tile, 1)],
                        win_key[:, bass.ds(w, 1)], ALU.subtract, ALU.is_equal).then_inc(hot_made, 1)

            dve.wait_ge(plan_made, 1)
            with dve.Fori(0, WPC) as w:
                window(w)

            for l in (1, 2, 3, 4):
                def scale_agg(c):
                    n, t = size_of(c)
                    if l == 1:
                        dve.wait_ge(agg_done[1], 3 * c + 1)
                        dve.wait_ge(rdeg_stored, 16 * c)
                        order.after(v.tensor_scalar(rdeg[:, 0:n], degree_ps[:, 0:n], 1.0, None, ALU.max))
                        v.reciprocal(rdeg[:, 0:n], rdeg[:, 0:n]).then_inc(rdeg_made, 1)
                        dve.wait_ge(rdeg_made, c + 1)
                    else:
                        dve.wait_ge(rdeg_loaded[l], 16 * (c + 1))
                    for h in range(AGG[l]):
                        dve.wait_ge(agg_done[l], 3 * (c + 1) if l == 1 else AGG[l] * (c + 1))
                        if h == 0:
                            dve.wait_ge(lin_done[l], LIN[l] * c)
                        v.scalar_tensor_tensor(out=aggT[:, h, 0:n], in0=agg_ps[:, h, 0:n],
                                               scalar=unscale[:, l - 1:l], in1=rdeg[:, 0:n], op0=ALU.mult,
                                               op1=ALU.mult).then_inc(agg_scaled[l], 1)

                def rest(c, next_c=None):
                    n, t = size_of(c)
                    if l == 2:
                        dve.wait_ge(lin_done[2], c + 1)
                        dve.wait_ge(hT_stored[2], 16 * c)
                        v.tensor_tensor(newT[:, 1, 0:n], lin_ps[:, 0, 0:n], aggT[:, 0, 0:n], ALU.add
                                        ).then_inc(summed, 1)
                        dve.wait_ge(summed, c + 1)
                    if next_c is not None:
                        scale_agg(next_c)
                    for h in range(TURNS[l]):
                        k = TURNS[l] * c + h
                        dve.wait_ge(high_done[l], k + 1)
                        v.scalar_tensor_tensor(out=partsT[:, 1, 0:n],
                                               in0=(lin_ps if l == 1 else newT)[:, h, 0:n],
                                               scalar=scale[:, l - 1:l], in1=partsT[:, 0, 0:n], op0=ALU.mult,
                                               op1=ALU.subtract).then_inc(low_done[l], 1)
                        dve.wait_ge(turned[l], k + 1)
                        if h == 0:
                            dve.wait_ge(H_stored[l], 16 * c)
                        q = P if n == CH else n
                        to = newH_flat(2 * F2 * TURNS[l])[0:q, 0:t, :].rearrange(
                            "p t (a f) -> p t a f", a=2)[:, :, :, h * P:(h + 1) * P]
                        v.tensor_copy(to, turn_ps[0:q, 0:2 * t, :].rearrange("p (t a) f -> p t a f", a=2)
                                      ).then_inc(turn_copied[l], 1)
                    if l == 4:
                        groups = ((0, 2), (2, 2)) if n == CH else ((0, 1),)
                        dve.wait_ge(x4_biased, TPC * c + t)
                        dve.wait_ge(out_stored, 16 * c)
                        q = P if n == CH else n
                        o = newT[:, :, :].rearrange("p a b -> p (a b)").rearrange("p (t f) -> p t f", t=TPC)
                        for g, (at, k) in enumerate(groups):
                            dve.wait_ge(lin_done[4], 2 * c + g + 1)
                            v.tensor_tensor(o[0:q, at:at + k, :],
                                            lin_ps[0:q, g, 0:k * D].rearrange("p (t f) -> p t f", t=k),
                                            x4[0:q, at:at + k, :], ALU.add).then_inc(out_made, 1)

                per_c = 1 if l == 1 else 0
                if l == 1:
                    with dve.Fori(0, WPC) as j:
                        window(WPC + j)
                    scale_agg(0)
                    with dve.Fori(1, NFULL - 1) as c:
                        with dve.Fori(0, WPC) as j:
                            window((c + 1) * WPC + j)
                        with order.rounds(c - 1, per_c, NFULL - 2):
                            rest(c - 1, c)
                    with dve.Fori(0, WTAIL) as j:
                        window(NFULL * WPC + j)
                    rest(NFULL - 2, NFULL - 1)
                else:
                    scale_agg(0)
                    with dve.Fori(1, NFULL) as c:
                        with order.rounds(c - 1, per_c, NFULL - 1):
                            rest(c - 1, c)
                rest(NFULL - 1, NFULL)
                rest(NFULL)

        @block.scalar
        def _(act):
            order = Order(act, act_order)
            a = nc.scalar
            act.wait_ge(consts_made, CONSTS)
            act.wait_ge(squares_summed, 1)
            a.activation(norms[:, 0:2, :], agg_ps[:, 0, :].rearrange("p (a n) -> p a n", a=2), ACT.Sqrt
                         ).then_inc(norms_made, 1)
            act.wait_ge(squares_summed, 2)
            a.activation(norms[:, 2:4, 0:F2], agg_ps[:, 0, 0:2 * F2].rearrange("p (a n) -> p a n", a=2), ACT.Sqrt
                         ).then_inc(norms_made, 1)
            act.wait_ge(squares_summed, 3)
            a.activation(norms[:, 4:6, :], agg_ps[:, 0, :].rearrange("p (a n) -> p a n", a=2), ACT.Sqrt
                         ).then_inc(norms_made, 1)
            act.wait_ge(norms_made, 4)
            a.activation(rownorm[:, 1:2], rownorm[:, 0:1], ACT.Sqrt).then_inc(norms_made, 1)
            act.wait_ge(norms_made, 6)
            a.activation(rownorm[:, 3:4], rownorm[:, 2:3], ACT.Sqrt).then_inc(norms_made, 1)

            def xbuf(slot):
                return (aggT if slot == 0 else selfT)[:, :, :].rearrange("p a b -> p (a b)").rearrange(
                    "p (t f) -> p t f", t=TPC)

            def h0_chunk(c, slot):
                n, t = size_of(c)
                act.wait_ge(moments_made, TPC * c + t)
                a.activation(rstd[:, 0:t], moments[:, 0:t, 1], ACT.Sqrt, bias=eps[:, 0:1]).then_inc(root_made, 1)
                act.wait_ge(shift_made, c + 1)
                for i in range(t):
                    a.activation(xbuf(slot)[:, i, :], xbuf(slot)[:, i, :], ACT.Relu, bias=shift[:, i:i + 1],
                                 scale=rstd[:, i:i + 1]).then_inc(h0_made, 1)
                act.wait_ge(h0_made, TPC * c + t)
                a.activation(H[:, bass.ds(c * TPC, t), 0, :], xbuf(slot)[:, 0:t, :], ACT.Copy, scale=H0_SCALE
                             ).then_inc(h0_high, 1)
                act.wait_ge(h0_turned, 2 * c + 2)
                act.wait_ge(hT_stored[0], 16 * c)
                nn = CH if n == CH else P
                a.activation(newT[:, 1, 0:nn], lin_ps[:, 1, 0:nn], ACT.Copy).then_inc(h0T_copied, 1)

            with act.Fori(0, NFULL // 2) as i:
                h0_chunk(2 * i, 0)
                h0_chunk(2 * i + 1, 1)
            h0_chunk(NFULL, 0)

            act.sem_inc(window_stored, 2)

            def store_window(w):
                act.wait_ge(window_counted, w + 1)
                a.activation(counts[:, :, bass.ds(w * WIN, WIN)],
                             window_ps[:, bass.ds(w & 1, 1), 0:KEYS].rearrange("p o (t w) -> p (o t) w", w=WIN),
                             ACT.Copy).then_inc(window_stored, 1)

            act.wait_ge(plan_made, 1)
            act.wait_ge(scales_made, 1)
            with act.Fori(0, WPC) as w:
                store_window(w)

            for l in (1, 2, 3, 4):
                def rest(c):
                    n, t = size_of(c)
                    if l == 4:
                        return
                    bias = {1: 0, 2: 2, 3: 3}[l]
                    act.wait_ge(hT_stored[l], 16 * c)
                    for h in range(NEW[l]):
                        if l == 2:
                            act.wait_ge(summed, c + 1)
                            source = newT[:, 1, 0:n]
                        else:
                            act.wait_ge(lin_done[l], NEW[l] * c + h + 1)
                            source = lin_ps[:, h, 0:n]
                        if l == 3:
                            act.wait_ge(low_done[3], 2 * c)
                        if l == 2:
                            act.wait_ge(low_done[2], c)
                        a.activation(newT[:, h, 0:n], source, ACT.Relu, bias=bT[:, bias + h:bias + h + 1]
                                     ).then_inc(relu_done[l], 1)
                    for h in range(TURNS[l]):
                        k = TURNS[l] * c + h
                        if l == 1:
                            act.wait_ge(narrow_done, c + 1)
                        else:
                            act.wait_ge(relu_done[l], NEW[l] * (c + 1))
                        act.wait_ge(turned[l], k)
                        a.activation(partsT[:, 0, 0:n], (lin_ps if l == 1 else newT)[:, h, 0:n], ACT.Copy,
                                     scale=scale[:, l - 1:l]).then_inc(high_done[l], 1)

                if l == 1:
                    with act.Fori(0, WPC) as j:
                        store_window(WPC + j)
                    with act.Fori(1, NFULL - 1) as c:
                        with act.Fori(0, WPC) as j:
                            store_window((c + 1) * WPC + j)
                        rest(c - 1)
                    with act.Fori(0, WTAIL) as j:
                        store_window(NFULL * WPC + j)
                    rest(NFULL - 2)
                elif l < 4:
                    with act.Fori(1, NFULL) as c:
                        rest(c - 1)
                if l < 4:
                    rest(NFULL - 1)
                    rest(NFULL)

        @block.tensor
        def _(pe):
            m = nc.tensor.matmul
            pe.wait_ge(consts_made, CONSTS)
            for a, rows_ in enumerate((within_f, key_f)):
                pe.wait_ge(edge_rows_ready, a + 1)
                for g in range(EG):
                    last = nc.tensor.transpose(window_ps[:, 1 - a, g * P:(g + 1) * P], rows_[:, g, :], ident32[:, :])
                last.then_inc(edges_turned, 1)
            ones = ones32

            def squares(k, views):
                pe.wait_ge(squares_made, k)
                if k > 1:
                    pe.wait_ge(norms_made, k - 1)
                for at, parts in views:
                    for i, part in enumerate(parts):
                        last = m(agg_ps[:, 0, at:at + part.shape[-1]], ones, part, start=(i == 0),
                                 stop=(i == len(parts) - 1))
                last.then_inc(squares_summed, 1)

            squares(1, [(D * i, [wsq[:, i, 0, :], wsq[:, i, 1, :]]) for i in range(2)])
            pe.wait_ge(ranges_found, 1)
            for i in range(2):
                for h in range(2):
                    at = 256 * i + h * WP
                    last = m(degree_ps[0:1, at:at + WP], lo_hi[0:WP, i, h:h + 1], ident32[0:WP, 0:WP], start=True,
                             stop=True)
            last.then_inc(ranges_turned, 1)
            squares(2, [(F2 * i, [wsq[:, i, 0, 0:F2], wsq[:, i, 1, 0:F2]]) for i in range(2)])
            squares(3, [(D * i, [wsq[:, 0, i, :]]) for i in range(2)])

            def xbuf(slot):
                return (aggT if slot == 0 else selfT)[:, :, :].rearrange("p a b -> p (a b)").rearrange(
                    "p (t f) -> p t f", t=TPC)

            def h0_chunk(c, slot):
                n, t = size_of(c)
                pe.wait_ge(h0_made, TPC * c + t)
                pe.wait_ge(h0T_copied, 2 * c)
                for f in range(2):
                    for i in range(t):
                        last = nc.tensor.transpose(lin_ps[:, f, i * P:(i + 1) * P],
                                                   xbuf(slot)[:, i, f * P:(f + 1) * P], ident32[:, :])
                    last.then_inc(h0_turned, 1)

            with pe.Fori(0, NFULL // 2) as i:
                h0_chunk(2 * i, 0)
                h0_chunk(2 * i + 1, 1)
            h0_chunk(NFULL, 0)

            pe.sem_inc(hot_free, RING)
            regs = [pe.alloc_register(f"pe_plan{i}") for i in range(3)]

            def window(w):
                first, steps, before = window_steps(pe, w, regs)
                pe.wait_ge(window_stored, w + 1)
                bank = window_ps[:, bass.ds(w & 1, 1), :]
                m(bank[:, :, KEYS:KEYS + 2], ones16[:, :], ones16[:, 0:2].unsqueeze(1), start=True, stop=False)
                with pe.Fori(0, steps) as i:
                    step = before + i
                    slot = step & (RING - 1)
                    pe.wait_ge(hot_made, 2 * step + 2)
                    m(bank[:, :, 0:KEYS], hot_src[:, bass.ds(slot, 1), :],
                      hot_key[:, bass.ds(slot, 1), :], start=False, stop=False).then_inc(hot_free, 1)
                m(bank[:, :, KEYS:KEYS + 2], ones16[:, :], ones16[:, 0:2].unsqueeze(1), start=False,
                  stop=True).then_inc(window_counted, 1)

            pe.wait_ge(plan_made, 1)
            with pe.Fori(0, WPC) as w:
                window(w)

            for l in (1, 2, 3, 4):
                H_of = H if AGG[l] == 2 else Hn

                def add_sources(c, k, first=False, final=False):
                    n, t = size_of(c)
                    kk = k if isinstance(k, int) else bass.ds(k, 1)
                    A = counts[:, kk, chunk_cols(c, n)]
                    if l == 1:
                        last = m(degree_ps[:, 0:n], ones16[:, :], A, start=first, stop=final)
                        if final:
                            last.then_inc(agg_done[1], 1)
                    for h in range(AGG[l]):
                        for part in range(2):
                            last = m(agg_ps[:, h, 0:n], H_of[:, kk, part, h * P:(h + 1) * P], A,
                                     start=first and part == 0, stop=final and part == 1)
                        if final:
                            last.then_inc(agg_done[l], 1)

                def open_agg(c):
                    if l == 1:
                        n, t = size_of(c)
                        pe.wait_ge(window_stored, 2 + (NWIN if n != CH else (c + 1) * WPC))
                    pe.wait_ge(agg_scaled[l], AGG[l] * c)
                    add_sources(c, 0, first=True)

                def agg(c):
                    open_agg(c)
                    with pe.Fori(1, NT - 1) as k:
                        add_sources(c, k)
                    add_sources(c, NT - 1, final=True)

                def agg_and_windows(c, n_windows):
                    first = (c + 1) * WPC
                    open_agg(c)
                    window(first)
                    with pe.Fori(1, NT - 1) as k:
                        window(first + k)
                        add_sources(c, k)
                    add_sources(c, NT - 1, final=True)
                    with pe.Fori(NT - 1, n_windows) as k:
                        window(first + k)

                def rest(c):
                    n, t = size_of(c)
                    pe.wait_ge(agg_scaled[l], AGG[l] * (c + 1))
                    pe.wait_ge(self_loaded[l], 16 * (c + 1))
                    if l in (1, 3):
                        for h in range(NEW[l]):
                            cols = slice(h * P, (h + 1) * P)
                            if l == 1:
                                ops = [(W14[:, 0, k, cols], aggT[:, k, 0:n]) for k in range(2)]
                                ops += [(W14[:, 1, k, cols], selfT[:, k, 0:n]) for k in range(2)]
                            else:
                                ops = [(W3[:, 0, cols], aggT[:, 0, 0:n]), (W3[:, 1, cols], selfT[:, 0, 0:n])]
                            for i, (w, r) in enumerate(ops):
                                last = m(lin_ps[:, h, 0:n], w, r, start=(i == 0), stop=(i == len(ops) - 1))
                            last.then_inc(lin_done[l], 1)
                    if l == 1:
                        pe.wait_ge(relu_done[1], 2 * (c + 1))
                        for k in range(2):
                            last = m(lin_ps[:, 0, 0:n], W2[:, 0, k, :], newT[:, k, 0:n], start=(k == 0),
                                     stop=(k == 1))
                        last.then_inc(narrow_done, 1)
                    if l == 2:
                        for k in range(2):
                            last = m(lin_ps[:, 0, 0:n], W2[:, 1, k, :], selfT[:, k, 0:n], start=(k == 0),
                                     stop=(k == 1))
                        last.then_inc(lin_done[2], 1)
                    for h in range(TURNS[l]):
                        k = TURNS[l] * c + h
                        pe.wait_ge(low_done[l], k + 1)
                        pe.wait_ge(turn_copied[l], k)
                        for i in range(t):
                            q = P if n == CH else n
                            for part in range(2):
                                last = nc.tensor.transpose(turn_ps[0:q, 2 * i + part, :],
                                                           partsT[:, part, i * P:i * P + q], ident16[:, :])
                        last.then_inc(turned[l], 1)
                    if l == 4:
                        pe.wait_ge(w4_loaded, 32)
                        pe.wait_ge(out_made, 2 * c)
                        for g in range(2 if n == CH else 1):
                            for i in range(2 if n == CH else 1):
                                q = P if n == CH else n
                                node = (2 * g + i) * P
                                ops = [(aggT[:, k, node:node + q], W14[:, 0, k, :]) for k in range(2)]
                                ops += [(selfT[:, k, node:node + q], W14[:, 1, k, :]) for k in range(2)]
                                for j, (h, w) in enumerate(ops):
                                    last = m(lin_ps[0:q, g, i * D:(i + 1) * D], h, w, start=(j == 0),
                                             stop=(j == len(ops) - 1))
                            last.then_inc(lin_done[4], 1)

                if l == 1:
                    pe.wait_ge(h0_low, NCH)
                    agg_and_windows(0, WPC)
                    with pe.Fori(1, NFULL - 1) as c:
                        agg_and_windows(c, WPC)
                        rest(c - 1)
                    with pe.Fori(0, WTAIL) as j:
                        window(NFULL * WPC + j)
                    agg(NFULL - 1)
                    rest(NFULL - 2)
                else:
                    for i in range(NFULL):
                        pe.wait_ge(H_loaded[i], 16 * (l - 1))
                        if i == 0:
                            add_sources(0, 0, first=True)
                        with pe.Fori(max(i * TPC, 1), (i + 1) * TPC) as k:
                            add_sources(0, k)
                    pe.wait_ge(H_loaded[NFULL], 16 * (l - 1))
                    add_sources(0, NT - 1, final=True)
                    with pe.Fori(1, NFULL) as c:
                        agg(c)
                        rest(c - 1)
                agg(NFULL)
                rest(NFULL - 1)
                rest(NFULL)


_INS = ['x', 'src', 'dst'] + [f'L0_gnn_{w}{i}' for i in (1, 2, 3, 4) for w in ('Wl', 'Wr', 'b')]


def kernel(**inputs):
    import numpy as _np
    import concourse.bacc as _bacc
    from concourse import mybir as _mybir
    from concourse.bass_utils import run_bass_kernel_spmd as _run

    nc = _bacc.Bacc("TRN2", target_bir_lowering=False, num_devices=1, dynamic_dma_scratch_size=1024)
    arrays, args = {}, []
    for name in _INS:
        a = _np.ascontiguousarray(inputs[name])
        arrays[f"in_{name}_dram"] = a
        args.append(nc.dram_tensor(f"in_{name}_dram", a.shape, _mybir.dt.from_np(a.dtype), kind="ExternalInput").ap())
    args.append(nc.dram_tensor("out_0_dram", inputs['x'].shape, _mybir.dt.float32, kind="ExternalOutput").ap())
    sage_stack_kernel(nc, *args)
    r = _run(nc, [arrays], core_ids=[0])
    return r.results[0]["out_0_dram"]
```

```python
import concourse.bass as bass
from concourse import mybir
from contextlib import ExitStack, contextmanager


class Order:

    def __init__(self, engine, semaphore):
        self.engine, self.semaphore, self.count, self.before = engine, semaphore, 0, 0

    def after(self, instruction):
        instruction.then_inc(self.semaphore, 1)
        self.count += 1
        self.engine.wait_ge(self.semaphore, self.before + self.count)

    @contextmanager
    def rounds(self, done_rounds, per_round, n_rounds):
        start = self.count
        self.before, self.count = done_rounds * per_round + start, 0
        yield
        assert self.count == per_round, (self.count, per_round)
        self.before, self.count = 0, start + per_round * n_rounds


def sage_stack_kernel(nc, x, src, dst, Wl1, Wr1, b1, Wl2, Wr2, b2, Wl3, Wr3, b3, Wl4, Wr4, b4, out):
    f32, f16, i32 = mybir.dt.float32, mybir.dt.float16, mybir.dt.int32
    ALU, ACT, AX = mybir.AluOpType, mybir.ActivationFunctionType, mybir.AxisListType

    P = 128
    N, D = x.shape
    E = src.shape[0]
    F2 = Wl2.shape[1]
    NT = -(-N // P)
    TAIL = N - (NT - 1) * P
    TPC = 4
    CH = TPC * P
    NFULL = (NT - 1) // TPC
    NCH = NFULL + 1
    assert NFULL * TPC == NT - 1 and 0 < TAIL <= P
    ET = -(-E // P)
    EG = -(-ET // P)
    WIN = 16
    NWIN = -(-N // WIN)
    WPC = CH // WIN
    WTAIL = NWIN - NFULL * WPC
    KEYS = WIN * NT
    NPAD = NWIN * WIN
    PAD_DST = NPAD - 1
    assert PAD_DST >= N
    WP = NWIN // 2
    assert WP * 2 == NWIN and WP <= P
    RING = 6
    BATCH = 4
    STEPS = [8 if w < 8 else 6 if w < 16 else 5 if w < 32 else 4 if w < 64 else 3 for w in range(NWIN)]
    STEP_AT = [sum(STEPS[:w]) for w in range(NWIN)]
    NSTEPS = sum(STEPS)
    RUNS = []
    for w, k in enumerate(STEPS):
        if not RUNS or RUNS[-1][2] != k:
            RUNS.append([w, 0, k])
        RUNS[-1][1] += 1
    TCOLS = ET + max(STEPS) + BATCH
    H0_SCALE = 2048.0
    FP16_ROOM = 32768.0
    EPS = 1e-5
    FAR = 1024.0

    ctx = ExitStack()
    with ctx:
        def sb(name, shape, dt):
            return ctx.enter_context(nc.sbuf_tensor(name, shape, dt))

        def pb(name, shape, dt):
            return ctx.enter_context(nc.psum_tensor(name, shape, dt))

        def sem(name):
            return ctx.enter_context(nc.semaphore(name))

        counts = sb("counts", [P, NT, NPAD], f16)
        H = sb("H", [P, NT, 2, D], f16)
        Hn = H[:, :, :, :].rearrange("p t h f -> p (t h f)")[:, 0:NT * 2 * F2].rearrange(
            "p (t h f) -> p t h f", t=NT, h=2)
        sizes = [RING * P, RING * KEYS] + [2 * n for n in (TCOLS, TCOLS, NSTEPS, NSTEPS)]
        early = sb("early", [P, sum(sizes)], f16)
        place = [sum(sizes[:i]) for i in range(len(sizes) + 1)]
        hot_src = early[:, place[0]:place[1]].rearrange("p (r n) -> p r n", r=RING)
        hot_key = early[:, place[1]:place[2]].rearrange("p (r n) -> p r n", r=RING)
        edge_src, edge_key, step_src, step_key = (
            early[:, place[i]:place[i + 1]].bitcast(f32) for i in (2, 3, 4, 5))
        late = early[:, 0:2 * (2 * D + 2 * F2 + D)].bitcast(f32)
        W3 = late[:, 0:2 * D].rearrange("p (a n) -> p a n", a=2)
        Wr2_sb = late[:, 2 * D:2 * D + 2 * F2].rearrange("p (k n) -> p k n", k=2)
        b4rows = late[:, 2 * D + 2 * F2:2 * D + 2 * F2 + D]
        plan = sb("plan", [1, NWIN, 2], i32)
        heavy = sb("heavy", [1, NCH], i32)
        W14 = sb("W14", [P, 2, 2, D], f32)
        Wl2_sb = sb("Wl2_sb", [P, 2, F2], f32)
        aggT = sb("aggT", [P, 2, CH], f32)
        selfT = sb("selfT", [P, 2, CH], f32)
        newT = sb("newT", [P, 2, CH], f32)
        partsT = sb("partsT", [P, 2, CH], f16)
        newH = sb("newH", [P, TPC, 2, D], f16)
        rdeg = sb("rdeg", [P, CH], f32)
        ident16 = sb("ident16", [P, P], f16)
        ident32 = sb("ident32", [P, P], f32)
        ones16 = sb("ones16", [P, P], f16)
        bT = sb("bT", [P, 5], f32)
        scale = sb("scale", [P, 3], f32)
        unscale = sb("unscale", [P, 4], f32)
        stats = sb("stats", [P, TPC, 6], f32)
        moments = sb("moments", [P, TPC, 2], f32)
        rstd = sb("rstd", [P, TPC], f32)
        shift = sb("shift", [P, TPC], f32)
        eps = sb("eps", [P, 1], f32)
        upper = newH[:, TPC // 2:TPC, :, :].rearrange("p t h f -> p (t h f)")
        src_numbers = upper[:, 0:P]
        key_numbers = upper[:, P:P + KEYS]
        win_key = upper[:, P + KEYS:P + KEYS + 2 * NWIN].bitcast(f32)

        spare = counts[:, :, :].rearrange("p t n -> p (t n)").bitcast(f32)
        taken = [0]

        def scratch(*shape):
            size = 1
            for s in shape:
                size *= s
            at = spare[:, taken[0]:taken[0] + size]
            taken[0] += size
            if len(shape) == 2:
                at = at.rearrange("p (a b) -> p a b", a=shape[0])
            if len(shape) == 3:
                at = at.rearrange("p (a b c) -> p a b c", a=shape[0], b=shape[1])
            return at

        src_rows = scratch(EG, P).bitcast(i32)
        dst_rows = scratch(EG, P).bitcast(i32)
        tile_rows = scratch(EG, P).bitcast(i32)
        within_rows = scratch(EG, P).bitcast(i32)
        dst_f = scratch(EG, P)
        tile_f = scratch(EG, P)
        within_f = scratch(EG, P)
        key_f = scratch(EG, P)
        span = scratch(2, EG)
        spans = scratch(2, EG * P)
        tile_up = scratch(EG * P)
        tile_down = scratch(EG * P)
        win_first = scratch(2)
        win_last = scratch(2)
        meets = scratch(2, EG * P)
        meets_b = scratch(2, EG * P)
        picked = scratch(2, EG * P)
        lo_far = scratch(2)
        lo_hi = scratch(2, 2)
        rows = scratch(2, 2, WP)
        lengths = scratch(NWIN)
        first_tiles = scratch(NWIN)
        more_tiles = scratch(NWIN)
        rounds_f = scratch(NWIN)
        rounds_i = scratch(NWIN).bitcast(i32)
        heavy_up = scratch(NWIN)
        heavy_f = scratch(NCH)
        steps_row = scratch(NWIN)
        place_up = scratch(NWIN)
        step_number = scratch(NSTEPS)
        step_win_key = scratch(NSTEPS)
        step_tile = scratch(NSTEPS)
        tile_number = scratch(EG)
        chosen = scratch(EG, NSTEPS)
        W3s = scratch(2, D)
        Wr2s = scratch(2, F2)
        ones32 = scratch(P)
        wsq = scratch(2, 2, D)
        norms = scratch(6, D)
        bias_rows = scratch(3, D)
        bound = scratch(D)
        bound_b = scratch(D)
        sq_row = scratch(D)
        rownorm = scratch(4)
        tops = scratch(3)

        window_ps = pb("window_ps", [P, 2, 512], f32)
        degree_ps = pb("degree_ps", [P, 512], f32)
        agg_ps = pb("agg_ps", [P, 2, 512], f32)
        lin_ps = pb("lin_ps", [P, 2, 512], f32)
        turn_ps = pb("turn_ps", [P, 2 * TPC, P], f16)

        span_d = nc.dram_tensor("span_d", [2, EG, P], f32, kind="Internal").ap()
        rdeg_d = nc.dram_tensor("rdeg_d", [1, NCH * CH], f32, kind="Internal").ap()
        hT_d = [nc.dram_tensor(f"hT{i}_d", [P, 2, NCH * CH], f32, kind="Internal").ap() for i in range(4)]
        H_d = [None] + [nc.dram_tensor(f"H{i}_d", [P, NT, 2 * w], f16, kind="Internal").ap()
                        for i, w in ((1, F2), (2, F2), (3, D))]

        dve_order = sem("dve_order")
        act_order = sem("act_order")
        pool_order = sem("pool_order")
        pads_set = sem("pads_set")
        consts_made = sem("consts_made")
        edges_loaded = sem("edges_loaded")
        weights_loaded = sem("weights_loaded")
        spans_found = sem("spans_found")
        spans_stored = sem("spans_stored")
        spans_loaded = sem("spans_loaded")
        edge_rows_ready = sem("edge_rows_ready")
        edges_turned = sem("edges_turned")
        ranges_found = sem("ranges_found")
        ranges_turned = sem("ranges_turned")
        plan_made = sem("plan_made")
        squares_made = sem("squares_made")
        squares_summed = sem("squares_summed")
        norms_made = sem("norms_made")
        scales_made = sem("scales_made")
        x_loaded = [sem("x_loaded0"), sem("x_loaded1")]
        tail_cleared = sem("tail_cleared")
        moments_made = sem("moments_made")
        root_made = sem("root_made")
        shift_made = sem("shift_made")
        h0_made = sem("h0_made")
        h0_high = sem("h0_high")
        h0_low = sem("h0_low")
        h0_turned = sem("h0_turned")
        h0T_copied = sem("h0T_copied")
        hot_made = sem("hot_made")
        hot_used = sem("hot_used")
        window_counted = sem("window_counted")
        window_stored = sem("window_stored")
        batch_made = sem("batch_made")
        batch_used = sem("batch_used")
        heavy_counted = sem("heavy_counted")
        heavy_stored = sem("heavy_stored")
        steps_chosen = sem("steps_chosen")
        steps_turned = sem("steps_turned")
        step_tables = sem("step_tables")
        degree_done = sem("degree_done")
        late_loaded = sem("late_loaded")
        rdeg_made = sem("rdeg_made")
        rdeg_stored = sem("rdeg_stored")
        hT_stored = [sem(f"hT{i}_stored") for i in range(4)]
        L = range(5)
        self_loaded = [sem(f"self_loaded_{i}") for i in L]
        rdeg_loaded = [sem(f"rdeg_loaded_{i}") for i in L]
        agg_done = [sem(f"agg_done_{i}") for i in L]
        agg_scaled = [sem(f"agg_scaled_{i}") for i in L]
        lin_done = [sem(f"lin_done_{i}") for i in L]
        relu_done = [sem(f"relu_done_{i}") for i in L]
        high_done = [sem(f"high_done_{i}") for i in L]
        low_done = [sem(f"low_done_{i}") for i in L]
        turned = [sem(f"turned_{i}") for i in L]
        turn_copied = [sem(f"turn_copied_{i}") for i in L]
        H_stored = [sem(f"H_stored_{i}") for i in L]
        narrow_done = sem("narrow_done")
        summed = sem("summed")
        H_loaded = [sem(f"H_loaded_{i}") for i in range(NCH)]
        x4_loaded = sem("x4_loaded")
        x4_biased = sem("x4_biased")
        out_made = sem("out_made")
        out_stored = sem("out_stored")

        AGG = [0, 2, 1, 1, 2]
        SELF = [0, 2, 2, 1, 2]
        NEW = [0, 2, 1, 2, 2]
        TURNS = [0, 1, 1, 2, 0]
        LIN = [0, 2, 1, 2, 2]
        NW = 12
        CONSTS = 5 + 10 + 3 * len(RUNS)
        LATE = 16 * 6
        ORDER = [0, NFULL] + list(range(1, NFULL))
        assert NCH % 2 == 1 and NCH >= 5
        x4 = newH[:, :, :, :].rearrange("p t h f -> p (t h f)").bitcast(f32).rearrange("p (t f) -> p t f", t=TPC)
        FULL = (CH, TPC)
        LAST = (TAIL, 1)

        def newH_flat(width):
            return newH[:, :, :, :].rearrange("p t h f -> p (t h f)")[:, 0:TPC * width].rearrange(
                "p (t w) -> p t w", t=TPC)

        def chunk_at(q):
            return ORDER[q] if isinstance(q, int) else q - 1

        def size_of(c):
            return LAST if isinstance(c, int) and c == NFULL else FULL

        def both(q, full, last):
            return full * q - (full - last if not isinstance(q, int) or q > 1 else 0)

        def over_places(eng, do):
            do(1, 1)
            do(2, 0)
            with eng.Fori(1, NCH // 2) as i:
                do(2 * i + 1, 1)
                do(2 * i + 2, 0)

        def chunk_cols(c, n):
            return bass.ds(c * CH, n)

        def windows_of(c):
            return list(range(c * WPC, min((c + 1) * WPC, NWIN)))

        PHASES = {-1: [ORDER[0]], 0: [ORDER[1], ORDER[2]]}
        for q in range(1, NCH):
            PHASES[q] = [ORDER[q + 1]] if 2 <= q < NCH - 1 else []
        FILL = [w for q in range(-1, NCH) for c in PHASES[q] for w in windows_of(c)]
        FILL_AT = {w: i for i, w in enumerate(FILL)}
        HOT_AT = {w: sum(STEPS[v] for v in FILL[:i]) for i, w in enumerate(FILL)}

        def filled_after(q):
            return sum(len(windows_of(c)) for p in range(-1, q + 1) for c in PHASES[p])

        def hots_after(q):
            return sum(STEPS[w] for w in FILL[:filled_after(q)])

        RELU_AT, HIGH_AT, LOW_AT, DEGREE_AT, COPY_AT, SCALE_AT = 4, 11, 11, 16, 17, 27
        LIN_K, NARROW_K, TURN_K = 1, 8, 14

        block = ctx.enter_context(nc.Block())

        @block.sync
        def _(sp):
            sp.wait_ge(pads_set, 2)
            full = E // P // P * P
            more = E // P - full
            for rows_, edges in ((src_rows, src), (dst_rows, dst)):
                sp.dma_start(rows_[:, 0:full // P, :],
                             edges[0:full * P].rearrange("(g p e) -> p g e", p=P, e=P)).then_inc(edges_loaded, 16)
                sp.dma_start(rows_[0:more, full // P, :],
                             edges[full * P:(full + more) * P].rearrange("(p e) -> p e", e=P)
                             ).then_inc(edges_loaded, 16)
                rest = E - (full + more) * P
                sp.dma_start(rows_[more:more + 1, full // P, 0:rest],
                             edges[(full + more) * P:E].rearrange("(p e) -> p e", p=1)).then_inc(edges_loaded, 16)

            def load_x(c, slot):
                n, t = size_of(c)
                buf = (aggT if slot == 0 else selfT)[:, :, :].rearrange("p a b -> p (a b)").rearrange(
                    "p (t f) -> p t f", t=TPC)
                if n == CH:
                    sp.dma_start(buf, x_chunk(c)).then_inc(x_loaded[slot], 16)
                else:
                    sp.dma_start(buf[0:n, 0, :], x[c * CH:N, :]).then_inc(x_loaded[slot], 16)

            def x_chunk(c):
                return x[chunk_cols(c, CH), :].rearrange("(t p) f -> p t f", p=P)

            def store_h0T(c):
                n, t = size_of(c)
                sp.wait_ge(h0T_copied, 2 * (c + 1))
                sp.dma_start(hT_d[0][:, :, chunk_cols(c, n)], newT[:, :, 0:n]).then_inc(hT_stored[0], 16)

            load_x(0, 0)
            load_x(1, 1)
            nw = 0

            def small(dst_ap, src_ap, scattered=False):
                nonlocal nw
                nw += 1
                sp.dma_start(dst_ap, src_ap, allow_slow_non_contiguous=scattered).then_inc(weights_loaded, 16)

            for i, w in enumerate((Wl1, Wr1)):
                small(W14[:, i, :, :], w.rearrange("(k p) n -> p k n", p=P))
            for i, w in enumerate((Wl2, Wr2)):
                small((Wl2_sb[:, :, :], Wr2s)[i], w.rearrange("(k p) n -> p k n", p=P))
            for i, w in enumerate((Wl3, Wr3)):
                small(W3s[:, i, :], w)
            small(bT[:, 0:2], b1.rearrange("(k p) -> p k", p=P), True)
            small(bT[:, 2:3], b2.rearrange("(k p) -> p k", p=P), True)
            small(bT[:, 3:5], b3.rearrange("(k p) -> p k", p=P), True)
            for i, b in enumerate((b1, b2, b3)):
                small(bias_rows[:, i, 0:b.shape[0]],
                      b.rearrange("(o n) -> o n", o=1).broadcast_to([P, b.shape[0]]))
            assert nw == NW

            sp.wait_ge(spans_found, 1)
            sp.dma_start(span_d.rearrange("a g p -> p a g"), span[:, :, :], allow_slow_non_contiguous=True
                         ).then_inc(spans_stored, 16)
            sp.wait_ge(spans_stored, 16)
            sp.dma_start(spans[:, :, :], span_d.rearrange("a g p -> a (g p)").unsqueeze(0).broadcast_to(
                [P, 2, EG * P])).then_inc(spans_loaded, 16)

            def pair(i):
                store_h0T(2 * i - 2)
                sp.wait_ge(h0_low, 2 * i - 1)
                load_x(2 * i, 0)
                store_h0T(2 * i - 1)
                sp.wait_ge(h0_low, 2 * i)
                load_x(2 * i + 1, 1)

            pair(1)
            with sp.Fori(2, NFULL // 2) as i:
                pair(i)
            store_h0T(NFULL - 2)
            sp.wait_ge(h0_low, NFULL - 1)
            sp.wait_ge(tail_cleared, 1)
            load_x(NFULL, 0)
            store_h0T(NFULL - 1)
            store_h0T(NFULL)

            for l in (1, 2, 3, 4):
                sp.wait_ge(hT_stored[l - 1], 16 * NCH)

                def load_self(q):
                    c = chunk_at(q)
                    n, t = size_of(c)
                    sp.dma_start(selfT[:, 0:SELF[l], 0:n], hT_d[l - 1][:, 0:SELF[l], chunk_cols(c, n)]
                                 ).then_inc(self_loaded[l], 16)

                def load_rdeg(q):
                    c = chunk_at(q)
                    n, t = size_of(c)
                    sp.dma_start(rdeg[:, 0:n], rdeg_d[0:1, chunk_cols(c, n)].broadcast_to([P, n])
                                 ).then_inc(rdeg_loaded[l], 16)

                def store_rdeg(q):
                    c = chunk_at(q)
                    n, t = size_of(c)
                    sp.wait_ge(rdeg_made, q + 1)
                    sp.dma_start(rdeg_d[0:1, chunk_cols(c, n)], rdeg[0:1, 0:n]).then_inc(rdeg_stored, 16)

                def store_new(q):
                    c = chunk_at(q)
                    n, t = size_of(c)
                    sp.wait_ge(relu_done[l], NEW[l] * (q + 1))
                    sp.dma_start(hT_d[l][:, 0:NEW[l], chunk_cols(c, n)], newT[:, 0:NEW[l], 0:n]
                                 ).then_inc(hT_stored[l], 16)

                def store_H(q):
                    c = chunk_at(q)
                    n, t = size_of(c)
                    sp.wait_ge(turn_copied[l], TURNS[l] * (q + 1))
                    sp.dma_start(H_d[l][:, bass.ds(c * TPC, t), :], newH_flat(2 * F2 * TURNS[l])[:, 0:t, :]
                                 ).then_inc(H_stored[l], 16)

                def store_out(q):
                    c = chunk_at(q)
                    n, t = size_of(c)
                    sp.wait_ge(out_made, both(q + 1, 2, 1))
                    o = newT[:, :, :].rearrange("p a b -> p (a b)").rearrange("p (t f) -> p t f", t=TPC)
                    if n == CH:
                        sp.dma_start(out[chunk_cols(c, CH), :].rearrange("(t p) f -> p t f", p=P), o
                                     ).then_inc(out_stored, 16)
                    else:
                        sp.dma_start(out[c * CH:N, :], o[0:n, 0, :]).then_inc(out_stored, 16)

                def load_x4(q):
                    c = chunk_at(q)
                    n, t = size_of(c)
                    if n == CH:
                        sp.dma_start(x4[:, :, :], x_chunk(c)).then_inc(x4_loaded, 16)
                    else:
                        sp.dma_start(x4[0:n, 0, :], x[c * CH:N, :]).then_inc(x4_loaded, 16)

                def after(q, last=False):
                    sp.wait_ge(lin_done[l], both(q + 1, LIN[l], 1 if l == 4 else LIN[l]))
                    if not last:
                        load_self(q + 1)
                        if l > 1:
                            sp.wait_ge(agg_scaled[l], AGG[l] * (q + 1))
                            load_rdeg(q + 1)
                    if l < 4:
                        store_new(q)
                        if l == 1 and not last:
                            store_rdeg(q + 1)
                        store_H(q)
                    else:
                        store_out(q)
                        if not last:
                            load_x4(q + 1)

                load_self(0)
                if l == 1:
                    store_rdeg(0)
                else:
                    if l == 2:
                        sp.wait_ge(rdeg_stored, 16 * NCH)
                    load_rdeg(0)
                if l == 2:
                    sp.dma_start(Wr2_sb, Wr2.rearrange("(k p) n -> p k n", p=P)).then_inc(late_loaded, 16)
                    for i, w in enumerate((Wl3, Wr3)):
                        sp.dma_start(W3[:, i, :], w).then_inc(late_loaded, 16)
                    sp.dma_start(b4rows, b4.rearrange("(o n) -> o n", o=1).broadcast_to([P, D])
                                 ).then_inc(late_loaded, 16)
                    for i, w in enumerate((Wl4, Wr4)):
                        sp.dma_start(W14[:, i, :, :], w.rearrange("(k p) n -> p k n", p=P)
                                     ).then_inc(late_loaded, 16)
                if l == 4:
                    load_x4(0)
                after(0)
                after(1)
                with sp.Fori(2, NCH - 2) as q:
                    after(q)
                after(NCH - 2)
                if l < 4:
                    sp.wait_ge(agg_done[l], AGG[l] * NCH)
                    sp.wait_ge(H_stored[l], 16 * (NCH - 1))
                    H_to = (H[:, :, :, :] if TURNS[l] == 2 else Hn).rearrange("p t h f -> p t (h f)")
                    for c in ORDER[:-1]:
                        a, b = c * TPC, c * TPC + size_of(c)[1]
                        sp.dma_start(H_to[:, a:b, :], H_d[l][:, a:b, :]).then_inc(H_loaded[c], 16)
                after(NCH - 1, last=True)
                if l < 4:
                    sp.wait_ge(H_stored[l], 16 * NCH)
                    a = ORDER[-1] * TPC
                    sp.dma_start(H_to[:, a:a + TPC, :], H_d[l][:, a:a + TPC, :]).then_inc(H_loaded[ORDER[-1]], 16)
            sp.wait_ge(out_stored, 16 * NCH)

        @block.gpsimd
        def _(pool):
            order = Order(pool, pool_order)
            nc.gpsimd.memset(src_rows[:, EG - 1, :], 0).then_inc(pads_set, 1)
            nc.gpsimd.memset(dst_rows[:, EG - 1, :], PAD_DST).then_inc(pads_set, 1)
            order.after(nc.gpsimd.memset(ident32[:, :], 0.0))
            order.after(nc.gpsimd.affine_select(out=ident32[:, :], in_=ident32[:, :], compare_op=ALU.not_equal,
                                                fill=1.0, base=0, pattern=[[-1, P]], channel_multiplier=1))
            nc.gpsimd.tensor_copy(ident16[:, :], ident32[:, :]).then_inc(consts_made, 1)
            nc.gpsimd.memset(ones16[:, :], 1.0).then_inc(consts_made, 1)
            nc.gpsimd.memset(ones32, 1.0).then_inc(consts_made, 1)
            nc.gpsimd.memset(eps[:, :], EPS).then_inc(consts_made, 1)
            nc.gpsimd.memset(unscale[:, 0:1], 1.0 / H0_SCALE).then_inc(consts_made, 1)

            n_numbers = 0

            def numbers(ap, pattern, base=0, rows=0):
                nonlocal n_numbers
                n_numbers += 1
                nc.gpsimd.iota(ap, pattern=pattern, base=base, channel_multiplier=rows,
                               allow_small_or_imprecise_dtypes=True).then_inc(consts_made, 1)

            numbers(src_numbers, [[1, P]])
            numbers(key_numbers, [[1, NT], [NT, WIN]])
            numbers(win_key, [[-KEYS, NWIN]])
            numbers(tile_up, [[1, EG * P]], base=1)
            numbers(tile_down, [[-1, EG * P]], base=int(FAR))
            numbers(win_first, [[WIN * WP, 2]], rows=WIN)
            numbers(win_last, [[WIN * WP, 2]], base=WIN - 1, rows=WIN)
            numbers(tile_number, [[P, EG]], rows=1)
            numbers(place_up[:, 0:NFULL * WPC], [[0, NFULL], [1, WPC]], base=1)
            numbers(place_up[:, NFULL * WPC:], [[1, WTAIL]], base=1)
            for w, n, k in RUNS:
                cols = slice(STEP_AT[w], STEP_AT[w] + n * k)
                numbers(step_number[:, cols], [[0, n], [1, k]])
                numbers(step_win_key[:, cols], [[-KEYS, n], [0, k]], base=-KEYS * w)
                numbers(steps_row[:, w:w + n], [[0, n]], base=k)
            assert n_numbers + 5 == CONSTS
            pool.wait_ge(late_loaded, LATE)

            def bias_x(q):
                n, t = size_of(chunk_at(q))
                pool.wait_ge(x4_loaded, 16 * (q + 1))
                for i in range(t):
                    q = P if n == CH else n
                    nc.gpsimd.tensor_tensor(x4[0:q, i, :], x4[0:q, i, :], b4rows[0:q, :], ALU.add
                                            ).then_inc(x4_biased, 1)

            bias_x(0)
            bias_x(1)
            with pool.Fori(2, NCH) as q:
                bias_x(q)

        def heavy_windows(eng, c, regs, do):
            eng.load(regs[0:1], heavy[0:1, c:c + 1])
            n_heavy = eng.snap(regs[0], min_val=0, max_val=WPC)
            with eng.If(n_heavy > 0):
                with eng.Fori(0, n_heavy) as i:
                    w = (c * WPC + i).with_bounds(min_val=0, max_val=NWIN - 1)
                    eng.load(regs[1:3], plan[0:1, bass.ds(w, 1), :])
                    do(w, eng.snap(regs[1], min_val=0, max_val=ET + max(STEPS)),
                       eng.snap(regs[2], min_val=1, max_val=ET))

        @block.vector
        def _(dve):
            order = Order(dve, dve_order)
            v = nc.vector
            dve.wait_ge(consts_made, CONSTS)
            dve.wait_ge(edges_loaded, 16 * 6)
            order.after(v.tensor_copy(dst_f, dst_rows))
            order.after(v.tensor_reduce(out=span[:, 0, :], in_=dst_f, axis=AX.X, op=ALU.min))
            v.tensor_reduce(out=span[:, 1, :], in_=dst_f, axis=AX.X, op=ALU.max).then_inc(spans_found, 1)
            order.after(v.tensor_single_scalar(tile_rows, src_rows, 7, ALU.logical_shift_right))
            order.after(v.tensor_single_scalar(within_rows, src_rows, P - 1, ALU.bitwise_and))
            order.after(v.tensor_copy(tile_f, tile_rows))
            v.tensor_copy(within_f, within_rows).then_inc(edge_rows_ready, 1)
            v.scalar_tensor_tensor(out=key_f, in0=dst_f, scalar=float(NT), in1=tile_f, op0=ALU.mult,
                                   op1=ALU.add).then_inc(edge_rows_ready, 1)
            dve.wait_ge(weights_loaded, 16 * NW)
            v.tensor_tensor(wsq[:, :, :, :], W14[:, :, :, :], W14[:, :, :, :], ALU.mult).then_inc(squares_made, 1)
            dve.wait_ge(edges_turned, 2)
            order.after(v.tensor_copy(edge_key, window_ps[:, 0, 0:TCOLS]))
            order.after(v.tensor_copy(edge_src, window_ps[:, 1, 0:TCOLS]))
            dve.wait_ge(spans_loaded, 16)
            for h in range(2):
                order.after(v.tensor_scalar(meets[0:WP, h, :], spans[0:WP, 0, :], win_last[0:WP, h:h + 1], None,
                                            ALU.is_le))
                order.after(v.scalar_tensor_tensor(out=meets_b[0:WP, h, :], in0=spans[0:WP, 1, :],
                                                   scalar=win_first[0:WP, h:h + 1], in1=meets[0:WP, h, :],
                                                   op0=ALU.is_ge, op1=ALU.mult))
                order.after(v.tensor_tensor(picked[0:WP, h, :], meets_b[0:WP, h, :], tile_up[0:WP, :], ALU.mult))
                order.after(v.tensor_reduce(out=lo_hi[0:WP, 1, h:h + 1], in_=picked[0:WP, h, :], axis=AX.X,
                                            op=ALU.max))
                order.after(v.tensor_tensor(picked[0:WP, h, :], meets_b[0:WP, h, :], tile_down[0:WP, :], ALU.mult))
                order.after(v.tensor_reduce(out=lo_far[0:WP, h:h + 1], in_=picked[0:WP, h, :], axis=AX.X,
                                            op=ALU.max))
            order.after(v.tensor_scalar(lo_hi[0:WP, 0, :], lo_far[0:WP, :], -1.0, FAR, ALU.mult, ALU.add))
            order.after(v.tensor_scalar(lo_hi[0:WP, 0, :], lo_hi[0:WP, 0, :], float(ET - 1), None, ALU.min))
            order.after(v.tensor_scalar(lo_far[0:WP, :], lo_hi[0:WP, 0, :], 1.0, None, ALU.add))
            order.after(v.tensor_scalar(lo_hi[0:WP, 1, :], lo_hi[0:WP, 1, :], float(ET), None, ALU.min))
            v.tensor_tensor(lo_hi[0:WP, 1, :], lo_hi[0:WP, 1, :], lo_far[0:WP, :], ALU.max).then_inc(ranges_found, 1)
            dve.wait_ge(ranges_turned, 1)
            for a in range(2):
                order.after(v.tensor_copy(rows[:, a, :, :], degree_ps[:, 256 * a:256 * a + 2 * WP].rearrange(
                    "p (h w) -> p h w", h=2)))
            lo_row = rows[:, 0, :, :].rearrange("p h w -> p (h w)")
            hi_row = rows[:, 1, :, :].rearrange("p h w -> p (h w)")
            for w, n, k in RUNS:
                cols = slice(STEP_AT[w], STEP_AT[w] + n * k)
                ins = v.tensor_tensor(step_tile[:, cols].rearrange("p (n k) -> p n k", k=k),
                                      lo_row[:, w:w + n].unsqueeze(2).broadcast_to([P, n, k]),
                                      step_number[:, cols].rearrange("p (n k) -> p n k", k=k), ALU.add)
            order.after(ins)
            for g in range(EG):
                ins = v.tensor_scalar(chosen[:, g, :], step_tile, tile_number[:, g:g + 1], None, ALU.is_equal)
            ins.then_inc(steps_chosen, 1)
            order.after(v.tensor_tensor(lengths, hi_row, lo_row, ALU.subtract))
            order.after(v.tensor_tensor(more_tiles, lengths, steps_row, ALU.subtract))
            order.after(v.tensor_scalar(rounds_f, more_tiles, float(BATCH - 1), float(BATCH), ALU.add, ALU.max))
            order.after(v.tensor_copy(rounds_i, rounds_f))
            order.after(v.tensor_single_scalar(rounds_i[0:1, :], rounds_i[0:1, :], BATCH.bit_length() - 1,
                                               ALU.logical_shift_right))
            v.tensor_copy(plan[0:1, :, 1], rounds_i[0:1, :]).then_inc(plan_made, 1)
            v.tensor_tensor(plan[0:1, :, 0], lo_row[0:1, :], steps_row[0:1, :], ALU.add).then_inc(plan_made, 1)
            order.after(v.scalar_tensor_tensor(out=heavy_up, in0=more_tiles, scalar=0.0, in1=place_up, op0=ALU.is_gt,
                                               op1=ALU.mult))
            v.tensor_reduce(out=heavy_f[:, 0:NFULL], in_=heavy_up[:, 0:NFULL * WPC].rearrange(
                "p (c w) -> p c w", w=WPC), axis=AX.X, op=ALU.max)
            order.after(v.tensor_reduce(out=heavy_f[:, NFULL:NCH], in_=heavy_up[:, NFULL * WPC:], axis=AX.X,
                                        op=ALU.max))
            v.tensor_copy(heavy[0:1, :], heavy_f[0:1, :]).then_inc(plan_made, 1)
            half = 512
            for a in range(2):
                dve.wait_ge(steps_turned, a + 1)
                for at in range(0, NSTEPS, half):
                    n = min(half, NSTEPS - at)
                    ps = (agg_ps, lin_ps)[a][:, at // half, 0:n]
                    if a == 0:
                        v.tensor_copy(step_src[:, at:at + n], ps).then_inc(step_tables, 1)
                    else:
                        v.tensor_tensor(step_key[:, at:at + n], ps, step_win_key[:, at:at + n], ALU.add
                                        ).then_inc(step_tables, 1)

            dve.wait_ge(squares_summed, 1)
            dve.wait_ge(norms_made, 1)
            v.tensor_tensor(wsq[:, 0, :, 0:F2], Wl2_sb[:, :, :], Wl2_sb[:, :, :], ALU.mult).then_inc(squares_made, 1)
            v.tensor_tensor(wsq[:, 1, :, 0:F2], Wr2s, Wr2s, ALU.mult).then_inc(squares_made, 1)
            dve.wait_ge(norms_made, 2)
            v.tensor_tensor(wsq[:, 0, :, :], W3s, W3s, ALU.mult).then_inc(squares_made, 1)
            dve.wait_ge(norms_made, 3)

            def row_norm(into, row):
                order.after(v.tensor_tensor(sq_row[:, 0:row.shape[-1]], row, row, ALU.mult))
                v.tensor_reduce(out=into, in_=sq_row[:, 0:row.shape[-1]], axis=AX.X, op=ALU.add
                                ).then_inc(norms_made, 1)

            root_d = float(D) ** 0.5
            order.after(v.tensor_tensor(bound, norms[:, 0, :], norms[:, 1, :], ALU.add))
            order.after(v.tensor_single_scalar(bound, bound, root_d, ALU.mult))
            order.after(v.scalar_tensor_tensor(out=bound_b, in0=bias_rows[:, 0, :], scalar=-1.0, in1=bias_rows[:, 0, :],
                                               op0=ALU.mult, op1=ALU.max))
            order.after(v.tensor_tensor(bound, bound, bound_b, ALU.add))
            row_norm(rownorm[:, 0:1], bound)
            dve.wait_ge(norms_made, 5)
            b2_ = bound[:, 0:F2]
            order.after(v.tensor_scalar(b2_, norms[:, 2, 0:F2], rownorm[:, 1:2], None, ALU.mult))
            order.after(v.tensor_reduce(out=tops[:, 0:1], in_=b2_, axis=AX.X, op=ALU.max))
            order.after(v.scalar_tensor_tensor(out=b2_, in0=norms[:, 3, 0:F2], scalar=rownorm[:, 1:2], in1=b2_,
                                               op0=ALU.mult, op1=ALU.add))
            order.after(v.scalar_tensor_tensor(out=bound_b[:, 0:F2], in0=bias_rows[:, 1, 0:F2], scalar=-1.0, in1=bias_rows[:, 1, 0:F2],
                                               op0=ALU.mult, op1=ALU.max))
            order.after(v.tensor_tensor(b2_, b2_, bound_b[:, 0:F2], ALU.add))
            order.after(v.tensor_reduce(out=tops[:, 1:2], in_=b2_, axis=AX.X, op=ALU.max))
            row_norm(rownorm[:, 2:3], b2_)
            dve.wait_ge(norms_made, 7)
            order.after(v.tensor_tensor(bound, norms[:, 4, :], norms[:, 5, :], ALU.add))
            order.after(v.tensor_scalar(bound, bound, rownorm[:, 3:4], None, ALU.mult))
            order.after(v.scalar_tensor_tensor(out=bound_b, in0=bias_rows[:, 2, :], scalar=-1.0, in1=bias_rows[:, 2, :],
                                               op0=ALU.mult, op1=ALU.max))
            order.after(v.tensor_tensor(bound, bound, bound_b, ALU.add))
            order.after(v.tensor_reduce(out=tops[:, 2:3], in_=bound, axis=AX.X, op=ALU.max))
            order.after(v.tensor_scalar(tops, tops, 1e-30, 1.0 / FP16_ROOM, ALU.max, ALU.mult))
            order.after(v.reciprocal(tops, tops))
            order.after(v.tensor_single_scalar(scale[:, :].bitcast(i32), tops.bitcast(i32), 0x7F800000,
                                               ALU.bitwise_and))
            v.reciprocal(unscale[:, 1:4], scale[:, :]).then_inc(scales_made, 1)

            def xbuf(slot):
                return (aggT if slot == 0 else selfT)[:, :, :].rearrange("p a b -> p (a b)").rearrange(
                    "p (t f) -> p t f", t=TPC)

            def h0_chunk(c, slot, uses):
                n, t = size_of(c)
                dve.wait_ge(x_loaded[slot], 16 * uses)
                for i in range(t):
                    v.bn_stats(stats[:, i, :], xbuf(slot)[:, i, :])
                dve.drain()
                for i in range(t):
                    v.bn_aggr(moments[:, i, :], stats[:, i, :]).then_inc(moments_made, 1)
                dve.wait_ge(root_made, c + 1)
                order.after(v.reciprocal(rstd[:, 0:t], rstd[:, 0:t]))
                v.scalar_tensor_tensor(out=shift[:, 0:t], in0=moments[:, 0:t, 0], scalar=-1.0, in1=rstd[:, 0:t],
                                       op0=ALU.mult, op1=ALU.mult).then_inc(shift_made, 1)
                dve.wait_ge(h0_high, c + 1)
                v.scalar_tensor_tensor(out=H[:, bass.ds(c * TPC, t), 1, :], in0=xbuf(slot)[:, 0:t, :],
                                       scalar=H0_SCALE, in1=H[:, bass.ds(c * TPC, t), 0, :], op0=ALU.mult,
                                       op1=ALU.subtract).then_inc(h0_low, 1)
                dve.wait_ge(h0_turned, 2 * c + 1)
                dve.wait_ge(hT_stored[0], 16 * c)
                nn = CH if n == CH else P
                v.tensor_copy(newT[:, 0, 0:nn], lin_ps[:, 0, 0:nn]).then_inc(h0T_copied, 1)

            per = 1
            def pair(i):
                h0_chunk(2 * i - 2, 0, i)
                h0_chunk(2 * i - 1, 1, i)

            pair(1)
            with dve.Fori(2, NFULL // 2 + 1) as i:
                with order.rounds(i - 2, 2 * per, NFULL // 2 - 1):
                    pair(i)
            dve.wait_ge(h0T_copied, 2 * (NFULL - 1))
            v.memset(xbuf(0)[:, 0, :], 0.0).then_inc(tail_cleared, 1)
            h0_chunk(NFULL, 0, NFULL // 2 + 1)

            regs = [dve.alloc_register(f"dve_plan{i}") for i in range(3)]
            batches = dve.alloc_register("dve_batches")
            dve.reg_mov(batches, 0)

            def window(w):
                for i in range(STEPS[w]):
                    at = HOT_AT[w] + i
                    step = STEP_AT[w] + i
                    if at >= RING:
                        dve.wait_ge(hot_used, at - RING + 1)
                    v.tensor_scalar(hot_src[:, at % RING, :], src_numbers, step_src[:, step:step + 1], None,
                                    ALU.is_equal)
                    v.tensor_scalar(hot_key[:, at % RING, :], key_numbers, step_key[:, step:step + 1], None,
                                    ALU.is_equal).then_inc(hot_made, 1)

            def heavy_of(q):
                if PHASES[q]:
                    dve.wait_ge(hot_used, hots_after(q))

                def rounds(w, first, n):
                    with dve.Fori(0, n) as r:
                        made = dve.snap(batches, min_val=0, max_val=NWIN * ET)
                        dve.wait_ge(batch_used, made + 1)
                        for j in range(BATCH):
                            tile = (first + BATCH * r + j).with_bounds(min_val=0, max_val=TCOLS - 1)
                            v.tensor_scalar(hot_src[:, j, :], src_numbers, edge_src[:, bass.ds(tile, 1)], None,
                                            ALU.is_equal)
                            last = v.tensor_scalar(hot_key[:, j, :], key_numbers, edge_key[:, bass.ds(tile, 1)],
                                                   win_key[:, bass.ds(w, 1)], ALU.subtract, ALU.is_equal)
                        last.then_inc(batch_made, 1)
                        dve.reg_add(batches, batches, 1)

                for c in PHASES[q]:
                    heavy_windows(dve, c, regs, rounds)
                if PHASES[q]:
                    dve.wait_ge(batch_used, dve.snap(batches, min_val=0, max_val=NWIN * ET) + 1)

            def scale_agg(l, q, bank):
                n, t = size_of(chunk_at(q))
                if l > 1:
                    dve.wait_ge(rdeg_loaded[l], 16 * (q + 1))
                if not isinstance(q, int) or q > 0:
                    dve.wait_ge(lin_done[l], both(q, LIN[l], 1 if l == 4 else LIN[l]))
                for h in range(AGG[l]):
                    dve.wait_ge(agg_done[l], AGG[l] * q + h + 1)
                    v.scalar_tensor_tensor(out=aggT[:, h, 0:n], in0=(agg_ps, window_ps)[bank][:, h, 0:n],
                                           scalar=unscale[:, l - 1:l], in1=rdeg[:, 0:n], op0=ALU.mult,
                                           op1=ALU.mult).then_inc(agg_scaled[l], 1)

            def low_part(l, q, h):
                n, t = size_of(chunk_at(q))
                dve.wait_ge(high_done[l], TURNS[l] * q + h + 1)
                v.scalar_tensor_tensor(out=partsT[:, 1, 0:n], in0=(lin_ps if l == 1 else newT)[:, h, 0:n],
                                       scalar=scale[:, l - 1:l], in1=partsT[:, 0, 0:n], op0=ALU.mult,
                                       op1=ALU.subtract).then_inc(low_done[l], 1)

            def copy_turned(l, q, h):
                n, t = size_of(chunk_at(q))
                dve.wait_ge(turned[l], TURNS[l] * q + h + 1)
                if h == 0 and (not isinstance(q, int) or q > 0):
                    dve.wait_ge(H_stored[l], 16 * q)
                rows_ = P if n == CH else n
                to = newH_flat(2 * F2 * TURNS[l])[0:rows_, 0:t, :].rearrange(
                    "p t (a f) -> p t a f", a=2)[:, :, :, h * P:(h + 1) * P]
                v.tensor_copy(to, turn_ps[0:rows_, 0:2 * t, :].rearrange("p (t a) f -> p t a f", a=2)
                              ).then_inc(turn_copied[l], 1)

            def degrees(q):
                n, t = size_of(chunk_at(q))
                dve.wait_ge(degree_done, q + 1)
                if q > 0:
                    dve.wait_ge(rdeg_stored, 16 * q)
                order.after(v.tensor_scalar(rdeg[:, 0:n], degree_ps[:, 0:n], 1.0, None, ALU.max))
                order.after(v.reciprocal(rdeg[:, 0:n], rdeg[:, 0:n]))
                dve.sem_inc(rdeg_made, 1)

            dve.wait_ge(step_tables, 2 * -(-NSTEPS // 512))
            for q in range(-1, NCH):
                between = {}
                if q >= 1:
                    between[LOW_AT] = [lambda: low_part(1, q - 1, 0)]
                    between[COPY_AT] = [lambda: copy_turned(1, q - 1, 0)]
                if q >= 0:
                    between.setdefault(DEGREE_AT, []).append(lambda: degrees(q))
                    between[SCALE_AT] = [lambda: scale_agg(1, q, 0)]
                ws = [w for c in PHASES[q] for w in windows_of(c)]
                for i in range(max(len(ws), SCALE_AT + 1)):
                    if i < len(ws):
                        window(ws[i])
                    for do in between.get(i, []):
                        do()
                heavy_of(q)
            low_part(1, NCH - 1, 0)
            copy_turned(1, NCH - 1, 0)

            def add_out(q):
                n, t = size_of(chunk_at(q))
                dve.wait_ge(x4_biased, both(q + 1, TPC, 1))
                if not isinstance(q, int) or q > 0:
                    dve.wait_ge(out_stored, 16 * q)
                rows_ = P if n == CH else n
                o = newT[:, :, :].rearrange("p a b -> p (a b)").rearrange("p (t f) -> p t f", t=TPC)
                for g, (at, k) in enumerate(((0, 2), (2, 2)) if n == CH else ((0, 1),)):
                    dve.wait_ge(lin_done[4], both(q, 2, 1) + g + 1)
                    v.tensor_tensor(o[0:rows_, at:at + k, :],
                                    lin_ps[0:rows_, g, 0:k * D].rearrange("p (t f) -> p t f", t=k),
                                    x4[0:rows_, at:at + k, :], ALU.add).then_inc(out_made, 1)

            for l in (2, 3, 4):
                def place(q, bank):
                    n, t = size_of(chunk_at(q))
                    scale_agg(l, q, bank)
                    if l == 2:
                        dve.wait_ge(lin_done[2], q + 1)
                        if not isinstance(q, int) or q > 0:
                            dve.wait_ge(hT_stored[2], 16 * q)
                        v.tensor_tensor(newT[:, 1, 0:n], lin_ps[:, 0, 0:n], aggT[:, 0, 0:n], ALU.add
                                        ).then_inc(summed, 1)
                    for h in range(TURNS[l]):
                        low_part(l, q, h)
                        copy_turned(l, q, h)
                    if l == 4:
                        add_out(q)

                place(0, 0)
                over_places(dve, place)

        @block.scalar
        def _(act):
            order = Order(act, act_order)
            a = nc.scalar
            act.wait_ge(consts_made, CONSTS)
            act.wait_ge(squares_summed, 1)
            a.activation(norms[:, 0:2, :], agg_ps[:, 0, :].rearrange("p (a n) -> p a n", a=2), ACT.Sqrt
                         ).then_inc(norms_made, 1)
            act.wait_ge(squares_summed, 2)
            a.activation(norms[:, 2:4, 0:F2], agg_ps[:, 0, 0:2 * F2].rearrange("p (a n) -> p a n", a=2), ACT.Sqrt
                         ).then_inc(norms_made, 1)
            act.wait_ge(squares_summed, 3)
            a.activation(norms[:, 4:6, :], agg_ps[:, 0, :].rearrange("p (a n) -> p a n", a=2), ACT.Sqrt
                         ).then_inc(norms_made, 1)
            act.wait_ge(norms_made, 4)
            a.activation(rownorm[:, 1:2], rownorm[:, 0:1], ACT.Sqrt).then_inc(norms_made, 1)
            act.wait_ge(norms_made, 6)
            a.activation(rownorm[:, 3:4], rownorm[:, 2:3], ACT.Sqrt).then_inc(norms_made, 1)

            def xbuf(slot):
                return (aggT if slot == 0 else selfT)[:, :, :].rearrange("p a b -> p (a b)").rearrange(
                    "p (t f) -> p t f", t=TPC)

            def h0_chunk(c, slot):
                n, t = size_of(c)
                act.wait_ge(moments_made, TPC * c + t)
                a.activation(rstd[:, 0:t], moments[:, 0:t, 1], ACT.Sqrt, bias=eps[:, 0:1]).then_inc(root_made, 1)
                act.wait_ge(shift_made, c + 1)
                for i in range(t):
                    a.activation(xbuf(slot)[:, i, :], xbuf(slot)[:, i, :], ACT.Relu, bias=shift[:, i:i + 1],
                                 scale=rstd[:, i:i + 1]).then_inc(h0_made, 1)
                act.wait_ge(h0_made, TPC * c + t)
                a.activation(H[:, bass.ds(c * TPC, t), 0, :], xbuf(slot)[:, 0:t, :], ACT.Copy, scale=H0_SCALE
                             ).then_inc(h0_high, 1)
                act.wait_ge(h0_turned, 2 * c + 2)
                act.wait_ge(hT_stored[0], 16 * c)
                nn = CH if n == CH else P
                a.activation(newT[:, 1, 0:nn], lin_ps[:, 1, 0:nn], ACT.Copy).then_inc(h0T_copied, 1)

            def pair(i):
                h0_chunk(2 * i - 2, 0)
                h0_chunk(2 * i - 1, 1)

            pair(1)
            with act.Fori(2, NFULL // 2 + 1) as i:
                pair(i)
            h0_chunk(NFULL, 0)

            def copy_window(w, bank, done):
                cols = slice(w * WIN, (w + 1) * WIN) if isinstance(w, int) else bass.ds(w * WIN, WIN)
                a.activation(counts[:, :, cols], window_ps[:, bank, 0:KEYS].rearrange("p (t w) -> p t w", w=WIN),
                             ACT.Copy).then_inc(done, 1)

            def store_window(w):
                act.wait_ge(window_counted, FILL_AT[w] + 1)
                copy_window(w, FILL_AT[w] % 2, window_stored)

            regs = [act.alloc_register(f"act_plan{i}") for i in range(3)]
            done_heavy = act.alloc_register("act_heavy")
            act.reg_mov(done_heavy, 0)

            def heavy_of(q):
                def store(w, first, n):
                    act.wait_ge(heavy_counted, act.snap(done_heavy, min_val=0, max_val=NWIN) + 1)
                    copy_window(w, 0, heavy_stored)
                    act.reg_add(done_heavy, done_heavy, 1)

                for c in PHASES[q]:
                    heavy_windows(act, c, regs, store)

            def relu(l, q):
                n, t = size_of(chunk_at(q))
                bias = {1: 0, 2: 2, 3: 3}[l]
                if not isinstance(q, int) or q > 0:
                    act.wait_ge(hT_stored[l], 16 * q)
                    act.wait_ge(low_done[l], TURNS[l] * q)
                for h in range(NEW[l]):
                    if l == 2:
                        act.wait_ge(summed, q + 1)
                        source = newT[:, 1, 0:n]
                    else:
                        act.wait_ge(lin_done[l], NEW[l] * q + h + 1)
                        source = lin_ps[:, h, 0:n]
                    a.activation(newT[:, h, 0:n], source, ACT.Relu, bias=bT[:, bias + h:bias + h + 1]
                                 ).then_inc(relu_done[l], 1)

            def high_part(l, q, h):
                n, t = size_of(chunk_at(q))
                if l == 1:
                    act.wait_ge(narrow_done, q + 1)
                else:
                    act.wait_ge(relu_done[l], NEW[l] * q + h + 1)
                if not (isinstance(q, int) and q == 0 and h == 0):
                    act.wait_ge(turned[l], TURNS[l] * q + h)
                a.activation(partsT[:, 0, 0:n], (lin_ps if l == 1 else newT)[:, h, 0:n], ACT.Copy,
                             scale=scale[:, l - 1:l]).then_inc(high_done[l], 1)

            act.wait_ge(step_tables, 2 * -(-NSTEPS // 512))
            act.wait_ge(plan_made, 3)
            act.wait_ge(scales_made, 1)
            for q in range(-1, NCH):
                between = {RELU_AT: lambda: relu(1, q - 1), HIGH_AT: lambda: high_part(1, q - 1, 0)}
                ws = [w for c in PHASES[q] for w in windows_of(c)]
                for i in range(max(len(ws), HIGH_AT + 1)):
                    if i < len(ws):
                        store_window(ws[i])
                    if i in between and q >= 1:
                        between[i]()
                heavy_of(q)
            relu(1, NCH - 1)
            high_part(1, NCH - 1, 0)

            for l in (2, 3):
                def place(q, bank):
                    relu(l, q)
                    for h in range(TURNS[l]):
                        high_part(l, q, h)

                place(0, 0)
                over_places(act, place)

        @block.tensor
        def _(pe):
            m = nc.tensor.matmul
            pe.wait_ge(consts_made, CONSTS)
            for a, rows_ in enumerate((within_f, key_f)):
                pe.wait_ge(edge_rows_ready, a + 1)
                for g in range(EG):
                    last = nc.tensor.transpose(window_ps[:, 1 - a, g * P:(g + 1) * P], rows_[:, g, :], ident32[:, :])
                last.then_inc(edges_turned, 1)
            ones = ones32

            def squares(made, k, views):
                pe.wait_ge(squares_made, made)
                if k > 1:
                    pe.wait_ge(norms_made, k - 1)
                for at, parts in views:
                    for i, part in enumerate(parts):
                        last = m(agg_ps[:, 0, at:at + part.shape[-1]], ones, part, start=(i == 0),
                                 stop=(i == len(parts) - 1))
                last.then_inc(squares_summed, 1)

            squares(1, 1, [(D * i, [wsq[:, i, 0, :], wsq[:, i, 1, :]]) for i in range(2)])
            pe.wait_ge(ranges_found, 1)
            for i in range(2):
                for h in range(2):
                    at = 256 * i + h * WP
                    last = m(degree_ps[:, at:at + WP], lo_hi[0:WP, i, h:h + 1].broadcast_to([WP, P]),
                             ident32[0:WP, 0:WP], start=True, stop=True)
            last.then_inc(ranges_turned, 1)
            pe.wait_ge(steps_chosen, 1)
            for a, rows_ in enumerate((within_f, key_f)):
                if a == 0:
                    pe.wait_ge(norms_made, 1)
                for at in range(0, NSTEPS, 512):
                    n = min(512, NSTEPS - at)
                    for g in range(EG):
                        last = m((agg_ps, lin_ps)[a][:, at // 512, 0:n], rows_[:, g, :], chosen[:, g, at:at + n],
                                 start=(g == 0), stop=(g == EG - 1))
                last.then_inc(steps_turned, 1)
            pe.wait_ge(step_tables, 2 * -(-NSTEPS // 512))
            squares(3, 2, [(F2 * i, [wsq[:, i, 0, 0:F2], wsq[:, i, 1, 0:F2]]) for i in range(2)])
            squares(4, 3, [(D * i, [wsq[:, 0, i, :]]) for i in range(2)])

            def xbuf(slot):
                return (aggT if slot == 0 else selfT)[:, :, :].rearrange("p a b -> p (a b)").rearrange(
                    "p (t f) -> p t f", t=TPC)

            def h0_chunk(c, slot):
                n, t = size_of(c)
                pe.wait_ge(h0_made, TPC * c + t)
                pe.wait_ge(h0T_copied, 2 * c)
                for f in range(2):
                    for i in range(t):
                        last = nc.tensor.transpose(lin_ps[:, f, i * P:(i + 1) * P],
                                                   xbuf(slot)[:, i, f * P:(f + 1) * P], ident32[:, :])
                    last.then_inc(h0_turned, 1)

            def pair(i):
                h0_chunk(2 * i - 2, 0)
                h0_chunk(2 * i - 1, 1)

            pair(1)
            with pe.Fori(2, NFULL // 2 + 1) as i:
                pair(i)
            h0_chunk(NFULL, 0)

            def open_window(bank):
                m(window_ps[:, bank, KEYS:KEYS + 2], ones16[:, :], ones16[:, 0:2], start=True, stop=False)

            def close_window(bank, done):
                m(window_ps[:, bank, KEYS:KEYS + 2], ones16[:, :], ones16[:, 0:2], start=False,
                  stop=True).then_inc(done, 1)

            def window(w):
                at = FILL_AT[w]
                if at >= 2:
                    pe.wait_ge(window_stored, at - 1)
                open_window(at % 2)
                for i in range(STEPS[w]):
                    k = HOT_AT[w] + i
                    pe.wait_ge(hot_made, k + 1)
                    m(window_ps[:, at % 2, 0:KEYS], hot_src[:, k % RING, :], hot_key[:, k % RING, :],
                      start=False, stop=False).then_inc(hot_used, 1)
                close_window(at % 2, window_counted)

            regs = [pe.alloc_register(f"pe_plan{i}") for i in range(3)]
            batches = pe.alloc_register("pe_batches")
            done_heavy = pe.alloc_register("pe_heavy")
            pe.reg_mov(batches, 0)
            pe.reg_mov(done_heavy, 0)
            pe.sem_inc(batch_used, 1)
            pe.sem_inc(heavy_stored, 1)

            def heavy_of(q):
                if PHASES[q]:
                    pe.wait_ge(window_stored, filled_after(q))

                def add(w, first, n):
                    pe.wait_ge(heavy_stored, pe.snap(done_heavy, min_val=0, max_val=NWIN) + 1)
                    open_window(0)
                    m(window_ps[:, 0, 0:KEYS].rearrange("p (t w) -> p t w", w=WIN), ident16[:, :],
                      counts[:, :, bass.ds(w * WIN, WIN)], start=False, stop=False)
                    with pe.Fori(0, n):
                        pe.wait_ge(batch_made, pe.snap(batches, min_val=0, max_val=NWIN * ET) + 1)
                        for j in range(BATCH):
                            last = m(window_ps[:, 0, 0:KEYS], hot_src[:, j, :], hot_key[:, j, :], start=False,
                                     stop=False)
                        last.then_inc(batch_used, 1)
                        pe.reg_add(batches, batches, 1)
                    close_window(0, heavy_counted)
                    pe.reg_add(done_heavy, done_heavy, 1)

                for c in PHASES[q]:
                    heavy_windows(pe, c, regs, add)
                if PHASES[q]:
                    pe.wait_ge(heavy_stored, pe.snap(done_heavy, min_val=0, max_val=NWIN) + 1)

            def lin(l, q):
                n, t = size_of(chunk_at(q))
                pe.wait_ge(agg_scaled[l], AGG[l] * (q + 1))
                pe.wait_ge(self_loaded[l], 16 * (q + 1))
                if l == 4:
                    if not isinstance(q, int) or q > 0:
                        pe.wait_ge(out_made, both(q, 2, 1))
                    for g in range(2 if n == CH else 1):
                        for i in range(2 if n == CH else 1):
                            rows_ = P if n == CH else n
                            node = (2 * g + i) * P
                            ops = [(aggT[:, k, node:node + rows_], W14[:, 0, k, :]) for k in range(2)]
                            ops += [(selfT[:, k, node:node + rows_], W14[:, 1, k, :]) for k in range(2)]
                            for j, (h, w) in enumerate(ops):
                                last = m(lin_ps[0:rows_, g, i * D:(i + 1) * D], h, w, start=(j == 0),
                                         stop=(j == len(ops) - 1))
                        last.then_inc(lin_done[4], 1)
                    return
                if l > 1 and (not isinstance(q, int) or q > 0):
                    pe.wait_ge(relu_done[l], NEW[l] * q)
                for h in range(1 if l == 2 else 2):
                    cols = slice(h * P, (h + 1) * P)
                    if l == 1:
                        ops = [(W14[:, 0, k, cols], aggT[:, k, 0:n]) for k in range(2)]
                        ops += [(W14[:, 1, k, cols], selfT[:, k, 0:n]) for k in range(2)]
                    elif l == 2:
                        ops = [(Wr2_sb[:, k, :], selfT[:, k, 0:n]) for k in range(2)]
                    else:
                        ops = [(W3[:, 0, cols], aggT[:, 0, 0:n]), (W3[:, 1, cols], selfT[:, 0, 0:n])]
                    for i, (w, r) in enumerate(ops):
                        last = m(lin_ps[:, h, 0:n], w, r, start=(i == 0), stop=(i == len(ops) - 1))
                    last.then_inc(lin_done[l], 1)

            def narrow(q):
                n, t = size_of(chunk_at(q))
                pe.wait_ge(relu_done[1], 2 * (q + 1))
                for k in range(2):
                    last = m(lin_ps[:, 0, 0:n], Wl2_sb[:, k, :], newT[:, k, 0:n], start=(k == 0), stop=(k == 1))
                last.then_inc(narrow_done, 1)

            def turn(l, q, h):
                n, t = size_of(chunk_at(q))
                pe.wait_ge(low_done[l], TURNS[l] * q + h + 1)
                if not (isinstance(q, int) and q == 0 and h == 0):
                    pe.wait_ge(turn_copied[l], TURNS[l] * q + h)
                rows_ = P if n == CH else n
                for i in range(t):
                    for part in range(2):
                        last = nc.tensor.transpose(turn_ps[0:rows_, 2 * i + part, :],
                                                   partsT[:, part, i * P:i * P + rows_], ident16[:, :])
                last.then_inc(turned[l], 1)

            def add_sources(l, q, bank, k, first, final):
                c = chunk_at(q)
                n, t = size_of(c)
                H_of = H if AGG[l] == 2 else Hn
                for h in range(AGG[l]):
                    for part in range(2):
                        last = m((agg_ps, window_ps)[bank][:, h, 0:n], H_of[:, k, part, h * P:(h + 1) * P],
                                 counts[:, k, chunk_cols(c, n)], start=first and part == 0,
                                 stop=final and part == 1)
                    if final:
                        last.then_inc(agg_done[l], 1)

            def add_degrees(q, k):
                c = chunk_at(q)
                n, t = size_of(c)
                last = m(degree_ps[:, 0:n], ones16[:, :], counts[:, k, chunk_cols(c, n)], start=(k == 0),
                         stop=(k == NT - 1))
                if k == NT - 1:
                    last.then_inc(degree_done, 1)

            for q in range(-1, NCH):
                ws = [w for c in PHASES[q] for w in windows_of(c)]
                if q == 0:
                    pe.wait_ge(h0_low, NCH)
                if q >= 0:
                    pe.wait_ge(window_stored, filled_after(q - 1) if q != 1 else filled_after(0))
                if q >= 1:
                    pe.wait_ge(rdeg_made, q)
                    pe.wait_ge(agg_scaled[1], 2 * q)
                for i in range(max(len(ws), NT)):
                    if q >= 0 and i < NT:
                        for k in range(2 * i, min(2 * i + 2, NT)):
                            add_degrees(q, k)
                        add_sources(1, q, 0, i, i == 0, i == NT - 1)
                    if q >= 1:
                        if i == LIN_K:
                            lin(1, q - 1)
                        if i == NARROW_K:
                            narrow(q - 1)
                        if i == TURN_K:
                            turn(1, q - 1, 0)
                    if i < len(ws):
                        window(ws[i])
                heavy_of(q)
            lin(1, NCH - 1)
            narrow(NCH - 1)
            turn(1, NCH - 1, 0)

            for l in (2, 3, 4):
                def rest(q):
                    if l == 4:
                        return {4: [lambda: lin(4, q)]}
                    if l == 3:
                        return {6: [lambda: lin(3, q)], 16: [lambda: turn(3, q, 0)], 22: [lambda: turn(3, q, 1)]}
                    return {6: [lambda: lin(2, q)], 18: [lambda: turn(2, q, 0)]}

                def place(q, bank):
                    between = rest(q - 1)
                    if not isinstance(q, int) or q > 1:
                        pe.wait_ge(agg_scaled[l], AGG[l] * (q - 1))
                    for k in range(NT):
                        add_sources(l, q, bank, k, k == 0, k == NT - 1)
                        for do in between.get(k, []):
                            do()

                pe.wait_ge(agg_scaled[l - 1], AGG[l - 1] * NCH)
                tiles = [(c, k) for c in ORDER for k in range(c * TPC, min((c + 1) * TPC, NT))]
                for i, (c, k) in enumerate(tiles):
                    pe.wait_ge(H_loaded[c], 16 * (l - 1))
                    add_sources(l, 0, 0, k, i == 0, i == NT - 1)
                if l == 2:
                    pe.wait_ge(late_loaded, LATE)
                over_places(pe, place)
                for fs in rest(NCH - 1).values():
                    for f in fs:
                        f()


_INS = ['x', 'src', 'dst'] + [f'L0_gnn_{w}{i}' for i in (1, 2, 3, 4) for w in ('Wl', 'Wr', 'b')]


def kernel(**inputs):
    import numpy as _np
    import concourse.bacc as _bacc
    from concourse import mybir as _mybir
    from concourse.bass_utils import run_bass_kernel_spmd as _run

    nc = _bacc.Bacc("TRN2", target_bir_lowering=False, num_devices=1, dynamic_dma_scratch_size=1024)
    arrays, args = {}, []
    for name in _INS:
        a = _np.ascontiguousarray(inputs[name])
        arrays[f"in_{name}_dram"] = a
        args.append(nc.dram_tensor(f"in_{name}_dram", a.shape, _mybir.dt.from_np(a.dtype), kind="ExternalInput").ap())
    args.append(nc.dram_tensor("out_0_dram", inputs['x'].shape, _mybir.dt.float32, kind="ExternalOutput").ap())
    sage_stack_kernel(nc, *args)
    r = _run(nc, [arrays], core_ids=[0])
    return r.results[0]["out_0_dram"]
```

```python
import concourse.bass as bass
from concourse import mybir
from contextlib import ExitStack, contextmanager


class Order:

    def __init__(self, engine, semaphore):
        self.engine, self.semaphore, self.count, self.before = engine, semaphore, 0, 0

    def after(self, instruction):
        instruction.then_inc(self.semaphore, 1)
        self.count += 1
        self.engine.wait_ge(self.semaphore, self.before + self.count)

    @contextmanager
    def rounds(self, done_rounds, per_round, n_rounds):
        start = self.count
        self.before, self.count = done_rounds * per_round + start, 0
        yield
        assert self.count == per_round, (self.count, per_round)
        self.before, self.count = 0, start + per_round * n_rounds


def sage_stack_kernel(nc, x, src, dst, Wl1, Wr1, b1, Wl2, Wr2, b2, Wl3, Wr3, b3, Wl4, Wr4, b4, out):
    f32, f16, bf16, i32 = mybir.dt.float32, mybir.dt.float16, mybir.dt.bfloat16, mybir.dt.int32
    ALU, ACT, AX = mybir.AluOpType, mybir.ActivationFunctionType, mybir.AxisListType

    P = 128
    N, D = x.shape
    E = src.shape[0]
    F2 = Wl2.shape[1]
    NT = -(-N // P)
    TAIL = N - (NT - 1) * P
    TPC = 4
    CH = TPC * P
    NFULL = (NT - 1) // TPC
    NCH = NFULL + 1
    assert NFULL * TPC == NT - 1 and 0 < TAIL <= P
    ET = -(-E // P)
    EG = -(-ET // P)
    WIN = 8
    PAIRS = -(-N // (2 * WIN))
    NWIN = 2 * PAIRS
    WPC = CH // WIN
    WTAIL = NWIN - NFULL * WPC
    KEYS = WIN * NT
    NPAD = NWIN * WIN
    PAD_DST = NPAD - 1
    assert PAD_DST >= N
    WCOLS = 4
    WP = NWIN // WCOLS
    assert WP * WCOLS == NWIN and WP <= P
    RING = 4
    GROUPS = 3
    BATCH = 4
    assert BATCH <= RING and GROUPS >= 2
    STEPS = ([20, 11, 9, 8, 7, 6, 6, 6] + [5] * 8 + [4] * 8 + [3] * 96 + [2] * NWIN)[:NWIN]

    def pairs_of(c):
        return list(range(c * WPC // 2, min((c + 1) * WPC // 2, PAIRS)))

    def steps_of(pairs):
        return sum(STEPS[2 * w] + STEPS[2 * w + 1] for w in pairs)

    ORDER = [NFULL - 1, NFULL] + list(range(NFULL - 2, -1, -1))
    assert NCH % 2 == 1 and NCH >= 5
    DUE = {-1: ORDER[0:1], 0: ORDER[1:3], **{q: [ORDER[q + 1]] for q in range(2, NCH - 2)}}
    FILLS = {q: [w for c in DUE.get(q, []) for w in pairs_of(c)] for q in range(-1, NCH)}
    spread = pairs_of(ORDER[-1])
    even = sum(steps_of(FILLS[q] + spread * (q == 0)) for q in range(0, NCH)) / (NCH - 2)
    for q in [0] + list(range(2, NCH - 2)):
        more = []
        while steps_of(FILLS[q] + more + spread[-1:]) <= even:
            more.insert(0, spread.pop())
        FILLS[q] += more
    FILLS[NCH - 2] = spread
    DUE[NCH - 2] = [ORDER[-1]]
    FILL = [w for q in range(-1, NCH) for w in FILLS[q]]
    FILL_AT = {w: i for i, w in enumerate(FILL)}
    HOT_AT = {w: steps_of(FILL[:FILL_AT[w]]) for w in FILL}
    NSTEPS = -(-sum(STEPS) // RING) * RING
    assert KEYS <= 256 and P <= KEYS
    assert NSTEPS <= 1024
    RUNS = []
    for w in (2 * pair + half for pair in FILL for half in range(2)):
        at = HOT_AT[w // 2] + STEPS[w - 1] * (w % 2)
        if not RUNS or RUNS[-1][2] != STEPS[w] or RUNS[-1][0] + RUNS[-1][1] != w:
            RUNS.append([w, 0, STEPS[w], at])
        RUNS[-1][1] += 1
    AHEAD = 2

    def script(q):
        steps = [("step", (w, i)) for w in FILLS[q] for i in range(steps_of([w]))]
        events, taken = [], 0
        for k in range(NT):
            for half, kind in enumerate(("sum", "half")):
                events.append((kind, k))
                upto = min(len(steps), -(-len(steps) * (2 * k + half + 1) // (2 * (NT - AHEAD))))
                events += steps[taken:upto]
                taken = upto
        return events + [("summed", NT - 1)]

    def filled_after(q):
        return sum(len(FILLS[p]) for p in range(-1, q + 1))

    def hots_after(q):
        return steps_of(FILL[:filled_after(q)])

    TCOLS = (ET + max(STEPS) + BATCH + 1) // 2 * 2
    H0_SCALE = 2048.0
    FP16_ROOM = 32768.0
    EPS = 1e-5
    FAR = 1024.0

    ctx = ExitStack()
    with ctx:
        def sb(name, shape, dt):
            return ctx.enter_context(nc.sbuf_tensor(name, shape, dt))

        def pb(name, shape, dt):
            return ctx.enter_context(nc.psum_tensor(name, shape, dt))

        def sem(name):
            return ctx.enter_context(nc.semaphore(name))

        counts = sb("counts", [P, NT, NPAD], f16)
        H = sb("H", [P, NT, 2, D], f16)
        Hn = H[:, :, :, :].rearrange("p t h f -> p (t h f)")[:, 0:NT * 2 * F2].rearrange(
            "p (t h f) -> p t h f", t=NT, h=2)
        sizes = [GROUPS * P * RING, GROUPS * KEYS * RING, KEYS * RING, TCOLS, NSTEPS, 2 * TCOLS, NSTEPS]
        early = sb("early", [P, sum(sizes)], f16)
        place = [sum(sizes[:i]) for i in range(len(sizes) + 1)]
        part = [early[:, place[i]:place[i + 1]] for i in range(len(sizes))]
        hot_src = part[0].rearrange("p (g n r) -> p g n r", g=GROUPS, r=RING)
        hot_key = part[1].rearrange("p (g n r) -> p g n r", g=GROUPS, r=RING)
        numbers_to = part[2].bitcast(bf16).rearrange("p (n r) -> p n r", r=RING)
        edge_src, step_src, step_key = (part[i].bitcast(bf16) for i in (3, 4, 6))
        edge_key = part[5].bitcast(f32)
        late = early[:, 0:2 * (2 * D + 2 * F2 + D)].bitcast(f32)
        W3 = late[:, 0:2 * D].rearrange("p (a n) -> p a n", a=2)
        Wr2_sb = late[:, 2 * D:2 * D + 2 * F2].rearrange("p (k n) -> p k n", k=2)
        b4rows = late[:, 2 * D + 2 * F2:2 * D + 2 * F2 + D]
        plan = sb("plan", [1, NWIN, 2], i32)
        heavy = sb("heavy", [1, NCH], i32)
        W14 = sb("W14", [P, 2, 2, D], f32)
        Wl2_sb = sb("Wl2_sb", [P, 2, F2], f32)
        aggT = sb("aggT", [P, 2, CH], f32)
        selfT = sb("selfT", [P, 2, CH], f32)
        newT = sb("newT", [P, 2, CH], f32)
        partsT = sb("partsT", [P, 2, CH], f16)
        newH = sb("newH", [P, TPC, 2, D], f16)
        rdeg = sb("rdeg", [P, CH], f32)
        ident16 = sb("ident16", [P, P], f16)
        columns = sb("columns", [P, 12], f32)
        bT = columns[:, 0:5]
        scale = columns[:, 5:8]
        unscale = columns[:, 8:12]
        upper = newH[:, TPC // 2:TPC, :, :].rearrange("p t h f -> p (t h f)")
        win_number = upper[:, 0:NWIN]
        ones16 = upper[:, NWIN:NWIN + P]
        uppers = upper[:, NWIN + P:NWIN + P + 2 * (3 * NCH * TPC + P + 1)].bitcast(f32)
        norm_parts = uppers[:, 0:2 * NCH * TPC].rearrange("p (a c t) -> p a c t", a=2, c=NCH)
        rdeg_columns = uppers[:, 2 * NCH * TPC:3 * NCH * TPC].rearrange("p (q t) -> p q t", t=TPC)
        ident32 = uppers[:, 3 * NCH * TPC:3 * NCH * TPC + P]
        heavy_key = uppers[:, 3 * NCH * TPC + P:]
        rstd, shift = norm_parts[:, 0, :, :], norm_parts[:, 1, :, :]

        def region(first, last, rows_):
            return taker([[k, first // 2, last // 2] for k in rows_])

        def taker(room):
            def take(*shape):
                size = 1
                for n in shape:
                    size *= n
                r = next(r for r in room if r[1] + size <= r[2])
                at = counts[:, r[0], :].bitcast(f32)[:, r[1]:r[1] + size]
                r[1] += size
                if len(shape) == 2:
                    at = at.rearrange("p (a b) -> p a b", a=shape[0])
                if len(shape) == 3:
                    at = at.rearrange("p (a b c) -> p a b c", a=shape[0], b=shape[1])
                return at
            return take

        XROWS = NCH
        x_in = [region(0, ORDER[2] * CH, [c])(TPC, D) for c in range(NCH)]
        lasting = region(CH, ORDER[2] * CH, range(XROWS, XROWS + 8))
        scratch = taker([[k, (ORDER[2] * CH if k < XROWS + 8 else 0) // 2, NPAD // 2] for k in range(NT)])

        meets = scratch(WCOLS * EG * P // 2).bitcast(f16).rearrange("p (h t) -> p h t", h=WCOLS)
        meets_b = scratch(WCOLS * EG * P // 2).bitcast(f16).rearrange("p (h t) -> p h t", h=WCOLS)
        picked = scratch(WCOLS * EG * P // 2).bitcast(f16).rearrange("p (h t) -> p h t", h=WCOLS)
        step_number = scratch(NSTEPS)
        step_win_key = scratch(NSTEPS)
        step_tile = scratch(NSTEPS // 2).bitcast(f16)
        chosen = [scratch(NSTEPS // 2).bitcast(f16) for _ in range(EG)]
        within_half, key_high, key_low = (scratch(EG * P // 2).bitcast(f16).rearrange("p (g e) -> p g e", g=EG)
                                          for _ in range(3))
        src_rows = scratch(EG, P).bitcast(i32)
        dst_rows = scratch(EG, P).bitcast(i32)
        tile_rows = scratch(EG, P).bitcast(i32)
        within_rows = scratch(EG, P).bitcast(i32)
        dst_f = scratch(EG, P)
        tile_f = scratch(EG, P)
        within_f = scratch(EG, P)
        key_f = scratch(EG, P)
        tile_up = scratch(EG * P // 2).bitcast(f16)
        tile_down = scratch(EG * P // 2).bitcast(f16)
        span = scratch(2, EG)
        win_first = scratch(WCOLS)
        win_last = scratch(WCOLS)
        lo_far = scratch(WCOLS)
        lo = scratch(WCOLS)
        hi = scratch(WCOLS)
        tile_number = scratch(EG)
        W3s = [lasting(D) for _ in range(2)]
        Wr2s = lasting(2, F2)
        ones32 = lasting(P)
        bias_rows = [lasting(D) for _ in range(3)]
        planning = region(CH + 2 * D, ORDER[2] * CH, range(XROWS + 2, XROWS + 8))
        lo_row = planning(NWIN)
        more_tiles = planning(NWIN)
        rounds_i = more_tiles.bitcast(i32)
        rounds_f = planning(NWIN)
        heavy_up = planning(NWIN)
        steps_row = planning(NWIN)
        place_up = planning(NWIN)
        heavy_f = planning(NCH)
        stats = planning(TPC, 6)
        moments = [planning(TPC, 2) for _ in range(NCH)]
        eps = planning(1)
        wsq1 = [lasting(2, D) for _ in range(2)]
        wsq2 = [lasting(2, F2) for _ in range(2)]
        wsq3 = [lasting(D) for _ in range(2)]
        norm1 = [lasting(D) for _ in range(2)]
        norm2 = [lasting(F2) for _ in range(2)]
        norm3 = [lasting(D) for _ in range(2)]
        bound = lasting(D)
        bound_b = lasting(D)
        sq_row = lasting(D)
        rownorm = lasting(4)
        tops = lasting(3)

        window_ps = pb("window_ps", [P, 2, 512], f32)
        degree_ps = pb("degree_ps", [P, 512], f32)
        agg_ps = pb("agg_ps", [P, 2, 512], f32)
        lin_ps = pb("lin_ps", [P, 2, 512], f32)
        turn_ps = pb("turn_ps", [P, 2 * TPC, P], f16)

        rdeg_d = nc.dram_tensor("rdeg_d", [1, NCH * CH], f32, kind="Internal").ap()
        hT_d = [nc.dram_tensor(f"hT{i}_d", [P, 2, NCH * CH], f32, kind="Internal").ap() for i in range(4)]
        H_d = [None] + [nc.dram_tensor(f"H{i}_d", [P, NT, 2 * w], f16, kind="Internal").ap()
                        for i, w in ((1, F2), (2, F2), (3, D))]

        dve_order = sem("dve_order")
        act_order = sem("act_order")
        pool_order = sem("pool_order")
        pads_set = sem("pads_set")
        consts_made = sem("consts_made")
        dst_loaded = sem("dst_loaded")
        src_loaded = sem("src_loaded")
        weights_loaded = sem("weights_loaded")
        spans_found = sem("spans_found")
        spans_turned = sem("spans_turned")
        edge_rows_ready = sem("edge_rows_ready")
        edge_halves = sem("edge_halves")
        edges_turned = sem("edges_turned")
        ranges_found = sem("ranges_found")
        ranges_turned = sem("ranges_turned")
        lo_copied = sem("lo_copied")
        plan_made = sem("plan_made")
        squares_made = sem("squares_made")
        squares_summed = sem("squares_summed")
        norms_made = sem("norms_made")
        rows_summed = sem("rows_summed")
        rows_rooted = sem("rows_rooted")
        edge_tables = sem("edge_tables")
        scales_made = sem("scales_made")
        x_loaded = [sem(f"x_loaded_{i}") for i in range(NCH)]
        tail_cleared = sem("tail_cleared")
        moments_made = sem("moments_made")
        root_made = sem("root_made")
        shift_made = sem("shift_made")
        h0_made = sem("h0_made")
        h0_high = sem("h0_high")
        h0_low = sem("h0_low")
        h0_turned = sem("h0_turned")
        h0T_copied = sem("h0T_copied")
        hot_made = sem("hot_made")
        hot_used = sem("hot_used")
        window_counted = sem("window_counted")
        window_stored = sem("window_stored")
        batch_made = sem("batch_made")
        batch_used = sem("batch_used")
        heavy_key_made = sem("heavy_key_made")
        heavy_counted = sem("heavy_counted")
        heavy_stored = sem("heavy_stored")
        steps_chosen = sem("steps_chosen")
        steps_turned = sem("steps_turned")
        step_tables = sem("step_tables")
        degree_done = sem("degree_done")
        degree_inverted = sem("degree_inverted")
        degree_turned = sem("degree_turned")
        late_loaded = sem("late_loaded")
        rdeg_made = sem("rdeg_made")
        rdeg_stored = sem("rdeg_stored")
        hT_stored = [sem(f"hT{i}_stored") for i in range(4)]
        L = range(5)
        self_loaded = [sem(f"self_loaded_{i}") for i in L]
        rdeg_loaded = [sem(f"rdeg_loaded_{i}") for i in L]
        agg_done = [sem(f"agg_done_{i}") for i in L]
        agg_scaled = [sem(f"agg_scaled_{i}") for i in L]
        lin_done = [sem(f"lin_done_{i}") for i in L]
        relu_done = [sem(f"relu_done_{i}") for i in L]
        high_done = [sem(f"high_done_{i}") for i in L]
        low_done = [sem(f"low_done_{i}") for i in L]
        turned = [sem(f"turned_{i}") for i in L]
        turn_copied = [sem(f"turn_copied_{i}") for i in L]
        H_stored = [sem(f"H_stored_{i}") for i in L]
        narrow_done = sem("narrow_done")
        summed = sem("summed")
        H_loaded = [sem(f"H_loaded_{i}") for i in range(NCH)]
        x4_loaded = sem("x4_loaded")
        x4_biased = sem("x4_biased")
        out_made = sem("out_made")
        out_stored = sem("out_stored")

        AGG = [0, 2, 1, 1, 2]
        SELF = [0, 2, 2, 1, 2]
        NEW = [0, 2, 1, 2, 2]
        TURNS = [0, 1, 1, 2, 0]
        LIN = [0, 2, 1, 2, 2]
        NW = 12
        CONSTS_TURN, CONSTS_RANGE = 1, 7
        CONSTS_STEPS = CONSTS_RANGE + 3 * len(RUNS) + 2
        CONSTS = CONSTS_STEPS + 8
        LATE = 16 * 6
        x4 = newH[:, :, :, :].rearrange("p t h f -> p (t h f)").bitcast(f32).rearrange("p (t f) -> p t f", t=TPC)
        FULL = (CH, TPC)
        LAST = (TAIL, 1)

        def newH_flat(width):
            return newH[:, :, :, :].rearrange("p t h f -> p (t h f)")[:, 0:TPC * width].rearrange(
                "p (t w) -> p t w", t=TPC)

        def chunk_at(q):
            return ORDER[q] if isinstance(q, int) else q * -1 + NFULL

        def size_of(c):
            return LAST if isinstance(c, int) and c == NFULL else FULL

        def both(q, full, last):
            return full * q - (full - last if not isinstance(q, int) or q > 1 else 0)

        def over_places(eng, do):
            do(1, 1)
            do(2, 0)
            with eng.Fori(1, NCH // 2) as i:
                do(2 * i + 1, 1)
                do(2 * i + 2, 0)

        def chunk_cols(c, n):
            return bass.ds(c * CH, n)

        LIN_K, NARROW_K, DEGREE_TURN_K, TURN_K = 2, 10, 12, 18
        RELU_K, HIGH_K, DEGREE_COPY_K = 4, 12, 13
        DEGREE_K, LOW_K, COPY_K = 0, 14, 20
        REST_AT = {1: (0, 4, 9), 2: (0, 8), 3: (0, 7, 11)}

        SLOTS = len(FILLS[-1]) // (NCH - 1)
        assert SLOTS >= 5

        block = ctx.enter_context(nc.Block())

        @block.sync
        def _(sp):
            full = E // P // P * P
            more = E // P - full
            rest = E - (full + more) * P
            for rows_, edges, loaded in ((dst_rows, dst, dst_loaded), (src_rows, src, src_loaded)):
                sp.dma_start(rows_[:, 0:full // P, :],
                             edges[0:full * P].rearrange("(g p e) -> p g e", p=P, e=P)).then_inc(loaded, 16)
                sp.wait_ge(pads_set, 2)
                sp.dma_start(rows_[0:more, full // P, :],
                             edges[full * P:(full + more) * P].rearrange("(p e) -> p e", e=P)
                             ).then_inc(loaded, 16)
                sp.dma_start(rows_[more:more + 1, full // P, 0:rest],
                             edges[(full + more) * P:E].rearrange("(p e) -> p e", p=1)).then_inc(loaded, 16)

            def load_x(c):
                n, t = size_of(c)
                if n == CH:
                    sp.dma_start(x_in[c], x_chunk(c)).then_inc(x_loaded[c], 16)
                else:
                    sp.wait_ge(tail_cleared, 1)
                    sp.dma_start(x_in[c][0:n, 0, :], x[c * CH:N, :]).then_inc(x_loaded[c], 16)

            def x_chunk(c):
                return x[chunk_cols(c, CH), :].rearrange("(t p) f -> p t f", p=P)

            def store_h0T(c):
                n, t = size_of(c)
                sp.wait_ge(h0T_copied, 2 * (c + 1))
                sp.dma_start(hT_d[0][:, :, chunk_cols(c, n)], newT[:, :, 0:n]).then_inc(hT_stored[0], 16)

            for c in range(NCH):
                load_x(c)
            nw = 0

            def small(dst_ap, src_ap, scattered=False):
                nonlocal nw
                nw += 1
                sp.dma_start(dst_ap, src_ap, allow_slow_non_contiguous=scattered).then_inc(weights_loaded, 16)

            for i, w in enumerate((Wl1, Wr1)):
                small(W14[:, i, :, :], w.rearrange("(k p) n -> p k n", p=P))
            for i, w in enumerate((Wl2, Wr2)):
                small((Wl2_sb[:, :, :], Wr2s)[i], w.rearrange("(k p) n -> p k n", p=P))
            for i, w in enumerate((Wl3, Wr3)):
                small(W3s[i], w)
            small(bT[:, 0:2], b1.rearrange("(k p) -> p k", p=P), True)
            small(bT[:, 2:3], b2.rearrange("(k p) -> p k", p=P), True)
            small(bT[:, 3:5], b3.rearrange("(k p) -> p k", p=P), True)
            for i, b in enumerate((b1, b2, b3)):
                small(bias_rows[i][:, 0:b.shape[0]],
                      b.rearrange("(o n) -> o n", o=1).broadcast_to([P, b.shape[0]]))
            assert nw == NW

            for c in range(NCH):
                store_h0T(c)

            for l in (1, 2, 3, 4):
                sp.wait_ge(hT_stored[l - 1], 16 * NCH)

                def load_self(q):
                    c = chunk_at(q)
                    n, t = size_of(c)
                    sp.dma_start(selfT[:, 0:SELF[l], 0:n], hT_d[l - 1][:, 0:SELF[l], chunk_cols(c, n)]
                                 ).then_inc(self_loaded[l], 16)

                def load_rdeg(q):
                    c = chunk_at(q)
                    n, t = size_of(c)
                    sp.dma_start(rdeg[:, 0:n], rdeg_d[0:1, chunk_cols(c, n)].broadcast_to([P, n])
                                 ).then_inc(rdeg_loaded[l], 16)

                def store_rdeg(q):
                    c = ORDER[q]
                    n, t = size_of(c)
                    rows_ = P if n == CH else n
                    sp.dma_start(rdeg_d[0, c * CH:c * CH + n].rearrange("(t p) -> p t", p=rows_),
                                 rdeg_columns[0:rows_, q, 0:t], allow_slow_non_contiguous=True
                                 ).then_inc(rdeg_stored, 16)

                def store_new(q):
                    c = chunk_at(q)
                    n, t = size_of(c)
                    sp.wait_ge(relu_done[l], NEW[l] * (q + 1))
                    sp.dma_start(hT_d[l][:, 0:NEW[l], chunk_cols(c, n)], newT[:, 0:NEW[l], 0:n]
                                 ).then_inc(hT_stored[l], 16)

                def store_H(q):
                    c = chunk_at(q)
                    n, t = size_of(c)
                    sp.wait_ge(turn_copied[l], TURNS[l] * (q + 1))
                    sp.dma_start(H_d[l][:, bass.ds(c * TPC, t), :], newH_flat(2 * F2 * TURNS[l])[:, 0:t, :]
                                 ).then_inc(H_stored[l], 16)

                def store_out(q):
                    c = chunk_at(q)
                    n, t = size_of(c)
                    sp.wait_ge(out_made, both(q + 1, 2, 1))
                    o = newT[:, :, :].rearrange("p a b -> p (a b)").rearrange("p (t f) -> p t f", t=TPC)
                    if n == CH:
                        sp.dma_start(out[chunk_cols(c, CH), :].rearrange("(t p) f -> p t f", p=P), o
                                     ).then_inc(out_stored, 16)
                    else:
                        sp.dma_start(out[c * CH:N, :], o[0:n, 0, :]).then_inc(out_stored, 16)

                def load_x4(q):
                    c = chunk_at(q)
                    n, t = size_of(c)
                    if n == CH:
                        sp.dma_start(x4[:, :, :], x_chunk(c)).then_inc(x4_loaded, 16)
                    else:
                        sp.dma_start(x4[0:n, 0, :], x[c * CH:N, :]).then_inc(x4_loaded, 16)

                def after(q, last=False):
                    sp.wait_ge(lin_done[l], both(q + 1, LIN[l], 1 if l == 4 else LIN[l]))
                    if not last:
                        load_self(q + 1)
                        if l > 1:
                            sp.wait_ge(agg_scaled[l], AGG[l] * (q + 1))
                            load_rdeg(q + 1)
                    if l < 4:
                        store_new(q)
                        store_H(q)
                    else:
                        store_out(q)
                        if not last:
                            load_x4(q + 1)

                load_self(0)
                if l > 1:
                    if l == 2:
                        sp.wait_ge(rdeg_stored, 16 * NCH)
                    load_rdeg(0)
                if l == 2:
                    sp.dma_start(Wr2_sb, Wr2.rearrange("(k p) n -> p k n", p=P)).then_inc(late_loaded, 16)
                    for i, w in enumerate((Wl3, Wr3)):
                        sp.dma_start(W3[:, i, :], w).then_inc(late_loaded, 16)
                    sp.dma_start(b4rows, b4.rearrange("(o n) -> o n", o=1).broadcast_to([P, D])
                                 ).then_inc(late_loaded, 16)
                    for i, w in enumerate((Wl4, Wr4)):
                        sp.dma_start(W14[:, i, :, :], w.rearrange("(k p) n -> p k n", p=P)
                                     ).then_inc(late_loaded, 16)
                if l == 4:
                    load_x4(0)
                after(0)
                after(1)
                with sp.Fori(2, NCH - 2) as q:
                    after(q)
                if l == 1:
                    sp.wait_ge(degree_inverted, NCH)
                    for q in range(NCH):
                        store_rdeg(q)
                after(NCH - 2)
                if l < 4:
                    sp.wait_ge(agg_done[l], AGG[l] * NCH)
                    sp.wait_ge(H_stored[l], 16 * (NCH - 1))
                    H_to = (H[:, :, :, :] if TURNS[l] == 2 else Hn).rearrange("p t h f -> p t (h f)")
                    for c in ORDER[:-1]:
                        a, b = c * TPC, c * TPC + size_of(c)[1]
                        sp.dma_start(H_to[:, a:b, :], H_d[l][:, a:b, :]).then_inc(H_loaded[c], 16)
                after(NCH - 1, last=True)
                if l < 4:
                    sp.wait_ge(H_stored[l], 16 * NCH)
                    a = ORDER[-1] * TPC
                    sp.dma_start(H_to[:, a:a + TPC, :], H_d[l][:, a:a + TPC, :]).then_inc(H_loaded[ORDER[-1]], 16)
            sp.wait_ge(out_stored, 16 * NCH)

        @block.gpsimd
        def _(pool):
            order = Order(pool, pool_order)
            nc.gpsimd.memset(src_rows[:, EG - 1, :], 0).then_inc(pads_set, 1)
            nc.gpsimd.memset(dst_rows[:, EG - 1, :], PAD_DST).then_inc(pads_set, 1)
            order.after(nc.gpsimd.memset(ident32[:, :], 0.0))
            nc.gpsimd.affine_select(out=ident32[:, :], in_=ident32[:, :], compare_op=ALU.not_equal,
                                    fill=1.0, base=0, pattern=[[-1, P]], channel_multiplier=1
                                    ).then_inc(consts_made, 1)
            made = 1
            assert made == CONSTS_TURN

            def numbers(ap, pattern, base=0, rows=0):
                nonlocal made
                made += 1
                nc.gpsimd.iota(ap, pattern=pattern, base=base, channel_multiplier=rows,
                               allow_small_or_imprecise_dtypes=True).then_inc(consts_made, 1)

            def fill(ap, value):
                nonlocal made
                made += 1
                nc.gpsimd.memset(ap, value).then_inc(consts_made, 1)

            fill(eps, EPS / H0_SCALE ** 2)
            numbers(win_first, [[WIN * WP, WCOLS]], rows=WIN)
            numbers(win_last, [[WIN * WP, WCOLS]], base=WIN - 1, rows=WIN)
            numbers(tile_up, [[1, EG * P]], base=1)
            numbers(tile_down, [[-1, EG * P]], base=int(FAR))
            numbers(tile_number, [[P, EG]], rows=1)
            assert made == CONSTS_RANGE
            for w, n, k, at in RUNS:
                cols = slice(at, at + n * k)
                numbers(step_number[:, cols], [[0, n], [1, k]])
                numbers(step_win_key[:, cols], [[-KEYS, n], [0, k]], base=-KEYS * w)
                numbers(steps_row[:, w:w + n], [[0, n]], base=k)
            idle = slice(sum(STEPS), NSTEPS)
            fill(step_tile[:, idle], 0.0)
            fill(step_win_key[:, idle], -float(KEYS * NWIN))
            assert made == CONSTS_STEPS
            numbers(numbers_to, [[1, KEYS], [0, RING]])
            numbers(win_number, [[1, NWIN]])
            numbers(place_up[:, 0:NFULL * WPC], [[0, NFULL], [1, WPC]], base=1)
            numbers(place_up[:, NFULL * WPC:], [[1, WTAIL]], base=1)
            fill(ones16[:, :], 1.0)
            fill(ones32, 1.0)
            fill(unscale[:, 0:1], 1.0 / H0_SCALE)
            pool.wait_ge(consts_made, made)
            made += 1
            nc.gpsimd.tensor_copy(ident16[:, :], ident32[:, :]).then_inc(consts_made, 1)
            assert made == CONSTS, (made, CONSTS)
            for c in range(NCH):
                n, t = size_of(c)
                tiles = slice(c * TPC, c * TPC + t)
                pool.wait_ge(h0_high, c + 1)
                nc.gpsimd.tensor_tensor(H[:, tiles, 1, :], x_in[c][:, 0:t, :], H[:, tiles, 0, :], ALU.subtract
                                        ).then_inc(h0_low, 1)
            pool.wait_ge(late_loaded, LATE)

            def bias_x(q):
                n, t = size_of(chunk_at(q))
                pool.wait_ge(x4_loaded, 16 * (q + 1))
                for i in range(t):
                    q = P if n == CH else n
                    nc.gpsimd.tensor_tensor(x4[0:q, i, :], x4[0:q, i, :], b4rows[0:q, :], ALU.add
                                            ).then_inc(x4_biased, 1)

            bias_x(0)
            bias_x(1)
            with pool.Fori(2, NCH) as q:
                bias_x(q)

        def heavy_group(q):
            return (hots_after(q) // RING + 1) % GROUPS

        def heavy_registers(eng, name):
            return ([eng.alloc_register(f"{name}_plan{i}") for i in range(2)],
                    [eng.alloc_register(f"{name}_heavy{c}") for c in range(NCH)])

        def load_heavy(eng, regs):
            eng.wait_ge(plan_made, 3)
            eng.load(regs[1], heavy[0:1, :])

        def heavy_windows(eng, c, regs, do):
            n_heavy = eng.snap(regs[1][c], min_val=0, max_val=WPC)
            with eng.If(n_heavy > 0):
                with eng.Fori(0, n_heavy) as i:
                    w = (c * WPC + i).with_bounds(min_val=0, max_val=NWIN - 1)
                    eng.load(regs[0], plan[0:1, bass.ds(w, 1), :])
                    do(w, eng.snap(regs[0][0], min_val=0, max_val=ET + max(STEPS)),
                       eng.snap(regs[0][1], min_val=1, max_val=ET))

        @block.vector
        def _(dve):
            order = Order(dve, dve_order)
            v = nc.vector
            v.memset(x_in[NFULL][:, 0, :], 0.0).then_inc(tail_cleared, 1)
            dve.wait_ge(dst_loaded, 16 * 3)
            order.after(v.tensor_copy(dst_f, dst_rows))
            v.tensor_reduce(out=span[:, 0, :], in_=dst_f, axis=AX.X, op=ALU.min)
            v.tensor_reduce(out=span[:, 1, :], in_=dst_f, axis=AX.X, op=ALU.max).then_inc(spans_found, 1)
            dve.wait_ge(src_loaded, 16 * 3)
            order.after(v.tensor_single_scalar(tile_rows, src_rows, 7, ALU.logical_shift_right))
            order.after(v.tensor_single_scalar(within_rows, src_rows, P - 1, ALU.bitwise_and))
            order.after(v.tensor_copy(tile_f, tile_rows))
            v.tensor_copy(within_f, within_rows).then_inc(edge_rows_ready, 1)
            v.scalar_tensor_tensor(out=key_f, in0=dst_f, scalar=float(NT), in1=tile_f, op0=ALU.mult,
                                   op1=ALU.add).then_inc(edge_rows_ready, 1)

            def h0_moments(c):
                n, t = size_of(c)
                dve.wait_ge(x_loaded[c], 16)
                if c > 0:
                    dve.wait_ge(moments_made, TPC * c)
                for i in range(t):
                    order.after(v.bn_stats(stats[:, i, :], x_in[c][:, i, :])) if i == t - 1 else v.bn_stats(
                        stats[:, i, :], x_in[c][:, i, :])
                for i in range(t):
                    v.bn_aggr(moments[c][:, i, :], stats[:, i, :]).then_inc(moments_made, 1)

            def h0_shift(c):
                n, t = size_of(c)
                dve.wait_ge(root_made, c + 1)
                order.after(v.reciprocal(rstd[:, c, 0:t], rstd[:, c, 0:t]))
                v.scalar_tensor_tensor(out=shift[:, c, 0:t], in0=moments[c][:, 0:t, 0], scalar=-1.0,
                                       in1=rstd[:, c, 0:t], op0=ALU.mult, op1=ALU.mult).then_inc(shift_made, 1)

            dve.wait_ge(spans_turned, 1)
            dve.wait_ge(consts_made, CONSTS_RANGE)
            tiles = (slice(0, WP), slice(0, WCOLS), slice(0, ET))
            for h in range(WCOLS):
                ins = v.tensor_scalar(meets[0:WP, h, 0:ET], lin_ps[0:WP, 0, 0:ET], win_last[0:WP, h:h + 1], None,
                                      ALU.is_le)
            order.after(ins)
            for h in range(WCOLS):
                ins = v.scalar_tensor_tensor(out=meets_b[0:WP, h, 0:ET], in0=lin_ps[0:WP, 1, 0:ET],
                                             scalar=win_first[0:WP, h:h + 1], in1=meets[0:WP, h, 0:ET],
                                             op0=ALU.is_ge, op1=ALU.mult)
            order.after(ins)
            order.after(v.tensor_tensor(meets[tiles], meets_b[tiles], tile_down[0:WP, 0:ET].unsqueeze(1).broadcast_to(
                [WP, WCOLS, ET]), ALU.mult))
            order.after(v.tensor_reduce(out=lo_far[0:WP, :], in_=meets[tiles], axis=AX.X, op=ALU.max))
            order.after(v.tensor_scalar(lo[0:WP, :], lo_far[0:WP, :], -1.0, FAR, ALU.mult, ALU.add))
            v.tensor_scalar(lo[0:WP, :], lo[0:WP, :], float(ET - 1), None, ALU.min).then_inc(ranges_found, 1)
            h0_moments(0)
            dve.wait_ge(edge_halves, 2)
            v.scalar_tensor_tensor(out=key_low, in0=key_f, scalar=0.5, in1=key_high, op0=ALU.mult,
                                   op1=ALU.subtract).then_inc(edge_halves, 1)
            dve.wait_ge(ranges_turned, 1)
            v.tensor_copy(lo_row, degree_ps[:, 0:NWIN]).then_inc(lo_copied, 1)
            dve.wait_ge(lo_copied, 1)
            dve.wait_ge(consts_made, CONSTS_STEPS)
            for w, n, k, at in RUNS:
                cols = slice(at, at + n * k)
                ins = v.tensor_tensor(step_tile[:, cols].rearrange("p (n k) -> p n k", k=k),
                                      lo_row[:, w:w + n].unsqueeze(2).broadcast_to([P, n, k]),
                                      step_number[:, cols].rearrange("p (n k) -> p n k", k=k), ALU.add)
            order.after(ins)
            for g in range(EG):
                ins = v.tensor_scalar(chosen[g], step_tile, tile_number[:, g:g + 1], 2.0, ALU.is_equal, ALU.mult)
            ins.then_inc(steps_chosen, 1)
            dve.wait_ge(edges_turned, 2)
            v.tensor_copy(edge_key, window_ps[:, 0, 0:TCOLS]).then_inc(edge_tables, 1)
            v.tensor_copy(edge_src, window_ps[:, 1, 0:TCOLS]).then_inc(edge_tables, 1)
            h0_shift(0)
            h0_moments(1)
            order.after(v.tensor_tensor(picked[tiles], meets_b[tiles], tile_up[0:WP, 0:ET].unsqueeze(1).broadcast_to(
                [WP, WCOLS, ET]), ALU.mult))
            v.tensor_reduce(out=hi[0:WP, :], in_=picked[tiles], axis=AX.X, op=ALU.max).then_inc(ranges_found, 1)

            def plan_heavy():
                dve.wait_ge(ranges_turned, 2)
                order.after(v.tensor_tensor(more_tiles, degree_ps[:, 0:NWIN], lo_row, ALU.subtract))
                order.after(v.tensor_tensor(more_tiles, more_tiles, steps_row, ALU.subtract))
                v.tensor_tensor(plan[0:1, :, 0], lo_row[0:1, :], steps_row[0:1, :], ALU.add).then_inc(plan_made, 1)
                order.after(v.tensor_scalar(rounds_f, more_tiles, float(BATCH - 1), float(BATCH), ALU.add, ALU.max))
                order.after(v.scalar_tensor_tensor(out=heavy_up, in0=more_tiles, scalar=0.0, in1=place_up,
                                                   op0=ALU.is_gt, op1=ALU.mult))
                order.after(v.tensor_copy(rounds_i, rounds_f))
                v.tensor_reduce(out=heavy_f[:, 0:NFULL], in_=heavy_up[:, 0:NFULL * WPC].rearrange(
                    "p (c w) -> p c w", w=WPC), axis=AX.X, op=ALU.max)
                order.after(v.tensor_reduce(out=heavy_f[:, NFULL:NCH], in_=heavy_up[:, NFULL * WPC:], axis=AX.X,
                                            op=ALU.max))
                v.tensor_copy(heavy[0:1, :], heavy_f[0:1, :]).then_inc(plan_made, 1)
                order.after(v.tensor_single_scalar(rounds_i[0:1, :], rounds_i[0:1, :], BATCH.bit_length() - 1,
                                                   ALU.logical_shift_right))
                v.tensor_copy(plan[0:1, :, 1], rounds_i[0:1, :]).then_inc(plan_made, 1)

            h0_shift(1)
            h0_moments(2)
            for a in range(2):
                dve.wait_ge(steps_turned, a + 1)
                for at in range(0, NSTEPS, 512):
                    n = min(512, NSTEPS - at)
                    ps = (agg_ps, window_ps)[a][:, at // 512, 0:n]
                    if a == 0:
                        ins = v.tensor_copy(step_src[:, at:at + n], ps)
                    else:
                        ins = v.tensor_tensor(step_key[:, at:at + n], ps, step_win_key[:, at:at + n], ALU.add)
                    ins.then_inc(step_tables, 1)

            def row_norm(into, row):
                order.after(v.tensor_tensor(sq_row[:, 0:row.shape[-1]], row, row, ALU.mult))
                v.tensor_reduce(out=into, in_=sq_row[:, 0:row.shape[-1]], axis=AX.X, op=ALU.add
                                ).then_inc(rows_summed, 1)

            def with_bias(width, i):
                order.after(v.scalar_tensor_tensor(out=bound_b[:, 0:width], in0=bias_rows[i][:, 0:width], scalar=-1.0,
                                                   in1=bias_rows[i][:, 0:width], op0=ALU.mult, op1=ALU.max))
                order.after(v.tensor_tensor(bound[:, 0:width], bound[:, 0:width], bound_b[:, 0:width], ALU.add))

            def square_weights():
                dve.wait_ge(weights_loaded, 16 * NW)
                for i in range(2):
                    v.tensor_tensor(wsq1[i], W14[:, i, :, :], W14[:, i, :, :], ALU.mult)
                    w2 = (Wl2_sb[:, :, :], Wr2s)[i]
                    v.tensor_tensor(wsq2[i], w2, w2, ALU.mult)
                    v.tensor_tensor(wsq3[i], W3s[i], W3s[i], ALU.mult).then_inc(squares_made, 1)

            def bound_h1():
                dve.wait_ge(norms_made, 1)
                order.after(v.tensor_tensor(bound, norm1[0], norm1[1], ALU.add))
                order.after(v.tensor_single_scalar(bound, bound, float(D) ** 0.5, ALU.mult))
                with_bias(D, 0)
                row_norm(rownorm[:, 0:1], bound)

            def bound_h2():
                dve.wait_ge(rows_rooted, 1)
                dve.wait_ge(norms_made, 2)
                b2_ = bound[:, 0:F2]
                order.after(v.tensor_scalar(b2_, norm2[0], rownorm[:, 1:2], None, ALU.mult))
                order.after(v.tensor_reduce(out=tops[:, 0:1], in_=b2_, axis=AX.X, op=ALU.max))
                order.after(v.scalar_tensor_tensor(out=b2_, in0=norm2[1], scalar=rownorm[:, 1:2], in1=b2_,
                                                   op0=ALU.mult, op1=ALU.add))
                with_bias(F2, 1)
                order.after(v.tensor_reduce(out=tops[:, 1:2], in_=b2_, axis=AX.X, op=ALU.max))
                row_norm(rownorm[:, 2:3], b2_)

            def bound_h3():
                dve.wait_ge(rows_rooted, 2)
                dve.wait_ge(norms_made, 3)
                order.after(v.tensor_tensor(bound, norm3[0], norm3[1], ALU.add))
                order.after(v.tensor_scalar(bound, bound, rownorm[:, 3:4], None, ALU.mult))
                with_bias(D, 2)
                order.after(v.tensor_reduce(out=tops[:, 2:3], in_=bound, axis=AX.X, op=ALU.max))
                order.after(v.tensor_scalar(tops, tops, 1e-30, 1.0 / FP16_ROOM, ALU.max, ALU.mult))
                order.after(v.reciprocal(tops, tops))
                order.after(v.tensor_single_scalar(scale[:, :].bitcast(i32), tops.bitcast(i32), 0x7F800000,
                                                   ALU.bitwise_and))
                v.reciprocal(unscale[:, 1:4], scale[:, :]).then_inc(scales_made, 1)

            regs = heavy_registers(dve, "dve")
            batches = dve.alloc_register("dve_batches")
            keys_made = dve.alloc_register("dve_keys")
            dve.reg_mov(batches, 0)
            dve.reg_mov(keys_made, 0)

            def step(w, i):
                at = HOT_AT[w] + i
                if at % RING > 0:
                    return
                group = at // RING
                if group >= GROUPS:
                    dve.wait_ge(hot_used, (group - GROUPS + 1) * RING)
                v.tensor_tensor(hot_src[:, group % GROUPS, :, :], numbers_to[:, 0:P, :],
                                step_src[:, at:at + RING].unsqueeze(1).broadcast_to([P, P, RING]), ALU.is_equal)
                v.tensor_tensor(hot_key[:, group % GROUPS, :, :], numbers_to,
                                step_key[:, at:at + RING].unsqueeze(1).broadcast_to([P, KEYS, RING]),
                                ALU.is_equal).then_inc(hot_made, 1)

            def heavy_of(q):
                if not DUE.get(q):
                    return
                done = hots_after(q)
                dve.wait_ge(hot_used, done)

                def rounds(w, first, n):
                    dve.wait_ge(batch_used, dve.snap(batches, min_val=0, max_val=NWIN * ET) + 1)
                    v.tensor_single_scalar(heavy_key, win_number[:, bass.ds(w, 1)], -float(KEYS), ALU.mult
                                           ).then_inc(heavy_key_made, 1)
                    dve.reg_add(keys_made, keys_made, 1)
                    with dve.Fori(0, n) as r:
                        made = dve.snap(batches, min_val=0, max_val=NWIN * ET) + 1
                        keys = dve.snap(keys_made, min_val=1, max_val=NWIN)
                        tile = (first + BATCH * r).with_bounds(min_val=0, max_val=TCOLS - BATCH)
                        dve.wait_ge(heavy_key_made, keys)
                        dve.wait_ge(batch_used, made)
                        v.tensor_tensor(hot_src[:, heavy_group(q), :, 0:BATCH], numbers_to[:, 0:P, 0:BATCH],
                                        edge_src[:, bass.ds(tile, BATCH)].unsqueeze(1).broadcast_to(
                                            [P, P, BATCH]), ALU.is_equal)
                        for j in range(BATCH):
                            last = v.tensor_scalar(hot_key[:, heavy_group(q), :, j], numbers_to[:, :, 0],
                                                   edge_key[:, bass.ds(tile + j, 1)], heavy_key, ALU.subtract,
                                                   ALU.is_equal)
                        last.then_inc(batch_made, 1)
                        dve.reg_add(batches, batches, 1)

                for c in DUE[q]:
                    heavy_windows(dve, c, regs, rounds)
                dve.wait_ge(batch_used, dve.snap(batches, min_val=0, max_val=NWIN * ET) + 1)

            def scale_agg(l, q, bank):
                n, t = size_of(chunk_at(q))
                if l > 1:
                    dve.wait_ge(rdeg_loaded[l], 16 * (q + 1))
                else:
                    dve.wait_ge(rdeg_made, q + 1)
                if not isinstance(q, int) or q > 0:
                    dve.wait_ge(lin_done[l], both(q, LIN[l], 1 if l == 4 else LIN[l]))
                for h in range(AGG[l]):
                    dve.wait_ge(agg_done[l], AGG[l] * q + h + 1)
                    v.scalar_tensor_tensor(out=aggT[:, h, 0:n], in0=(agg_ps, window_ps)[bank][:, h, 0:n],
                                           scalar=unscale[:, l - 1:l], in1=rdeg[:, 0:n], op0=ALU.mult,
                                           op1=ALU.mult).then_inc(agg_scaled[l], 1)

            def low_part(l, q, h):
                n, t = size_of(chunk_at(q))
                dve.wait_ge(high_done[l], TURNS[l] * q + h + 1)
                v.scalar_tensor_tensor(out=partsT[:, 1, 0:n], in0=(lin_ps if l == 1 else newT)[:, h, 0:n],
                                       scalar=scale[:, l - 1:l], in1=partsT[:, 0, 0:n], op0=ALU.mult,
                                       op1=ALU.subtract).then_inc(low_done[l], 1)

            def copy_turned(l, q, h):
                n, t = size_of(chunk_at(q))
                dve.wait_ge(turned[l], TURNS[l] * q + h + 1)
                if h == 0 and (not isinstance(q, int) or q > 0):
                    dve.wait_ge(H_stored[l], 16 * q)
                rows_ = P if n == CH else n
                to = newH_flat(2 * F2 * TURNS[l])[0:rows_, 0:t, :].rearrange(
                    "p t (a f) -> p t a f", a=2)[:, :, :, h * P:(h + 1) * P]
                v.tensor_copy(to, turn_ps[0:rows_, 0:2 * t, :].rearrange("p (t a) f -> p t a f", a=2)
                              ).then_inc(turn_copied[l], 1)

            def degrees(q):
                n, t = size_of(chunk_at(q))
                rows_ = P if n == CH else n
                dve.wait_ge(degree_done, q + 1)
                order.after(v.tensor_scalar(rdeg_columns[0:rows_, q, 0:t], lin_ps[0:rows_, 0, 0:2 * t].rearrange(
                    "p (t a) -> p t a", a=2)[:, :, 0], 1.0, None, ALU.max))
                v.reciprocal(rdeg_columns[0:rows_, q, 0:t], rdeg_columns[0:rows_, q, 0:t]).then_inc(degree_inverted, 1)

            dve.wait_ge(step_tables, 2 * -(-NSTEPS // 512))
            dve.wait_ge(consts_made, CONSTS)
            for i, w in enumerate(FILLS[-1]):
                c, turn = i // SLOTS + 1, i % SLOTS
                if i == 2:
                    plan_heavy()
                if turn == 1 and c + 1 < NCH:
                    h0_shift(c + 1)
                if turn == 3 and c + 2 < NCH:
                    h0_moments(c + 2)
                for j in range(steps_of([w])):
                    step(w, j)
            load_heavy(dve, regs)
            heavy_of(-1)
            for q in range(NCH):
                for kind, k in script(q):
                    if kind == "step":
                        step(*k)
                    if kind == "summed":
                        scale_agg(1, q, 0)
                    if kind != "sum":
                        continue
                    if q == 0 and k in (0, 6, 10, 14):
                        {0: square_weights, 6: bound_h1, 10: bound_h2, 14: bound_h3}[k]()
                    if k == DEGREE_K:
                        degrees(q)
                    if q >= 1 and k == LOW_K:
                        low_part(1, q - 1, 0)
                    if q >= 1 and k == COPY_K:
                        copy_turned(1, q - 1, 0)
                heavy_of(q)
            low_part(1, NCH - 1, 0)
            copy_turned(1, NCH - 1, 0)

            def add_out(q):
                n, t = size_of(chunk_at(q))
                dve.wait_ge(x4_biased, both(q + 1, TPC, 1))
                if not isinstance(q, int) or q > 0:
                    dve.wait_ge(out_stored, 16 * q)
                rows_ = P if n == CH else n
                o = newT[:, :, :].rearrange("p a b -> p (a b)").rearrange("p (t f) -> p t f", t=TPC)
                for g, (at, k) in enumerate(((0, 2), (2, 2)) if n == CH else ((0, 1),)):
                    dve.wait_ge(lin_done[4], both(q, 2, 1) + g + 1)
                    v.tensor_tensor(o[0:rows_, at:at + k, :],
                                    lin_ps[0:rows_, g, 0:k * D].rearrange("p (t f) -> p t f", t=k),
                                    x4[0:rows_, at:at + k, :], ALU.add).then_inc(out_made, 1)

            for l in (2, 3, 4):
                def place(q, bank):
                    n, t = size_of(chunk_at(q))
                    scale_agg(l, q, bank)
                    if l == 2:
                        dve.wait_ge(lin_done[2], q + 1)
                        if not isinstance(q, int) or q > 0:
                            dve.wait_ge(hT_stored[2], 16 * q)
                        v.tensor_tensor(newT[:, 1, 0:n], lin_ps[:, 0, 0:n], aggT[:, 0, 0:n], ALU.add
                                        ).then_inc(summed, 1)
                    for h in range(TURNS[l]):
                        low_part(l, q, h)
                        copy_turned(l, q, h)
                    if l == 4:
                        add_out(q)

                place(0, 0)
                over_places(dve, place)

        @block.scalar
        def _(act):
            order = Order(act, act_order)
            a = nc.scalar
            act.wait_ge(consts_made, 2)

            def h0_root(c):
                n, t = size_of(c)
                act.wait_ge(moments_made, TPC * c + t)
                a.activation(rstd[:, c, 0:t], moments[c][:, 0:t, 1], ACT.Sqrt, bias=eps[:, 0:1],
                             scale=H0_SCALE ** -2).then_inc(root_made, 1)

            def h0_relu(c, tiles):
                n, t = size_of(c)
                act.wait_ge(shift_made, c + 1)
                for i in tiles:
                    if i < t:
                        a.activation(x_in[c][:, i, :], x_in[c][:, i, :], ACT.Relu, bias=shift[:, c, i:i + 1],
                                     scale=rstd[:, c, i:i + 1]).then_inc(h0_made, 1)

            def h0_high_part(c):
                n, t = size_of(c)
                act.wait_ge(h0_made, TPC * c + t)
                a.activation(H[:, c * TPC:c * TPC + t, 0, :], x_in[c][:, 0:t, :], ACT.Copy).then_inc(h0_high, 1)

            def h0_copy(c, f):
                n, t = size_of(c)
                act.wait_ge(h0_turned, 2 * c + f + 1)
                if c > 0:
                    act.wait_ge(hT_stored[0], 16 * c)
                a.activation(newT[:, f, 0:t * P], lin_ps[:, f, 0:t * P], ACT.Copy, scale=1 / H0_SCALE
                             ).then_inc(h0T_copied, 1)

            def norms(i):
                into, width = ((norm1, D), (norm2, F2), (norm3, D))[i]
                act.wait_ge(squares_summed, i + 1)
                for j in range(2):
                    ins = a.activation(into[j], lin_ps[:, i % 2, j * width:(j + 1) * width], ACT.Sqrt)
                ins.then_inc(norms_made, 1)

            def root_row(i):
                act.wait_ge(rows_summed, i + 1)
                a.activation(rownorm[:, 2 * i + 1:2 * i + 2], rownorm[:, 2 * i:2 * i + 1], ACT.Sqrt
                             ).then_inc(rows_rooted, 1)

            def step(w, i):
                if i < steps_of([w]) - 1:
                    return
                act.wait_ge(window_counted, FILL_AT[w] + 1)
                a.activation(counts[:, :, 2 * w * WIN:2 * (w + 1) * WIN].rearrange("p t (a w) -> p a t w", a=2),
                             window_ps[:, FILL_AT[w] % 2, 0:2 * KEYS].rearrange("p (a w t) -> p a t w", a=2, w=WIN),
                             ACT.Copy).then_inc(window_stored, 1)

            regs = heavy_registers(act, "act")
            done_heavy = act.alloc_register("act_heavy")
            act.reg_mov(done_heavy, 0)

            def heavy_of(q):
                def store(w, first, n):
                    act.wait_ge(heavy_counted, act.snap(done_heavy, min_val=0, max_val=NWIN) + 1)
                    a.activation(counts[:, :, bass.ds(w * WIN, WIN)],
                                 window_ps[:, 0, 0:KEYS].rearrange("p (w t) -> p t w", w=WIN),
                                 ACT.Copy).then_inc(heavy_stored, 1)
                    act.reg_add(done_heavy, done_heavy, 1)

                for c in DUE.get(q, []):
                    heavy_windows(act, c, regs, store)

            def copy_degrees(q):
                n, t = size_of(chunk_at(q))
                act.wait_ge(degree_turned, q + 1)
                if q > 0:
                    act.wait_ge(agg_scaled[1], 2 * q)
                a.activation(rdeg[:, 0:n], degree_ps[:, 0:n], ACT.Copy).then_inc(rdeg_made, 1)

            def relu(l, q):
                n, t = size_of(chunk_at(q))
                bias = {1: 0, 2: 2, 3: 3}[l]
                if not isinstance(q, int) or q > 0:
                    act.wait_ge(hT_stored[l], 16 * q)
                    act.wait_ge(low_done[l], TURNS[l] * q)
                for h in range(NEW[l]):
                    if l == 2:
                        act.wait_ge(summed, q + 1)
                        source = newT[:, 1, 0:n]
                    else:
                        act.wait_ge(lin_done[l], NEW[l] * q + h + 1)
                        source = lin_ps[:, h, 0:n]
                    a.activation(newT[:, h, 0:n], source, ACT.Relu, bias=bT[:, bias + h:bias + h + 1]
                                 ).then_inc(relu_done[l], 1)

            def high_part(l, q, h):
                n, t = size_of(chunk_at(q))
                if l == 1:
                    act.wait_ge(narrow_done, q + 1)
                else:
                    act.wait_ge(relu_done[l], NEW[l] * q + h + 1)
                if not (isinstance(q, int) and q == 0 and h == 0):
                    act.wait_ge(turned[l], TURNS[l] * q + h)
                a.activation(partsT[:, 0, 0:n], (lin_ps if l == 1 else newT)[:, h, 0:n], ACT.Copy,
                             scale=scale[:, l - 1:l]).then_inc(high_done[l], 1)

            act.wait_ge(edge_rows_ready, 1)
            a.activation(within_half, within_f, ACT.Copy, scale=0.5).then_inc(edge_halves, 1)
            act.wait_ge(edge_rows_ready, 2)
            a.activation(key_high, key_f, ACT.Copy, scale=0.5).then_inc(edge_halves, 1)
            h0_root(0)
            for c in range(2):
                h0_relu(c, range(TPC))
                h0_high_part(c)
                h0_root(c + 1)
            for f in range(2):
                h0_copy(0, f)
            act.wait_ge(step_tables, 2 * -(-NSTEPS // 512))
            for i, w in enumerate(FILLS[-1]):
                c, turn = i // SLOTS + 1, i % SLOTS
                if turn < 2 and c < NCH:
                    h0_copy(c, turn)
                if turn in (2, 3) and c + 1 < NCH:
                    h0_relu(c + 1, range(TPC // 2 * (turn - 2), TPC // 2 * (turn - 1)))
                if turn == 4:
                    if c + 1 < NCH:
                        h0_high_part(c + 1)
                    if c + 2 < NCH:
                        h0_root(c + 2)
                step(w, steps_of([w]) - 1)
            load_heavy(act, regs)
            heavy_of(-1)
            for q in range(NCH):
                for kind, k in script(q):
                    if kind == "step":
                        step(*k)
                    if kind != "sum":
                        continue
                    if q == 0 and k in (4, 5, 9):
                        norms((4, 5, 9).index(k))
                    if k == DEGREE_COPY_K:
                        copy_degrees(q)
                    if q == 0 and k in (8, 12):
                        root_row((8, 12).index(k))
                    if q >= 1 and k == RELU_K:
                        relu(1, q - 1)
                    if q >= 1 and k == HIGH_K:
                        if q == 1:
                            act.wait_ge(scales_made, 1)
                        high_part(1, q - 1, 0)
                heavy_of(q)
            relu(1, NCH - 1)
            high_part(1, NCH - 1, 0)

            for l in (2, 3):
                def place(q, bank):
                    relu(l, q)
                    for h in range(TURNS[l]):
                        high_part(l, q, h)

                place(0, 0)
                over_places(act, place)

        @block.tensor
        def _(pe):
            m = nc.tensor.matmul
            pe.wait_ge(consts_made, CONSTS_TURN)
            pe.wait_ge(spans_found, 1)
            for a in range(2):
                for g in range(EG):
                    last = m(lin_ps[:, a, g * P:(g + 1) * P], span[:, a, g:g + 1].broadcast_to([P, P]), ident32[:, :],
                             start=True, stop=True)
            last.then_inc(spans_turned, 1)
            for a, rows_ in enumerate((within_f, key_f)):
                pe.wait_ge(edge_rows_ready, a + 1)
                for g in range(EG):
                    last = nc.tensor.transpose(window_ps[:, 1 - a, g * P:(g + 1) * P], rows_[:, g, :], ident32[:, :])
                last.then_inc(edges_turned, 1)
            def turn_range(column):
                for h in range(WCOLS):
                    last = m(degree_ps[:, h * WP:(h + 1) * WP], column[0:WP, h:h + 1].broadcast_to([WP, P]),
                             ident32[0:WP, 0:WP], start=True, stop=True)
                last.then_inc(ranges_turned, 1)

            pe.wait_ge(ranges_found, 1)
            turn_range(lo)

            def h0_turn(c):
                n, t = size_of(c)
                pe.wait_ge(h0_made, TPC * c + t)
                if c > 0:
                    pe.wait_ge(h0T_copied, 2 * c)
                for f in range(2):
                    for i in range(t):
                        last = nc.tensor.transpose(lin_ps[:, f, i * P:(i + 1) * P],
                                                   x_in[c][:, i, f * P:(f + 1) * P], ident32[:, :])
                    last.then_inc(h0_turned, 1)

            pe.wait_ge(steps_chosen, 1)
            pe.wait_ge(edge_tables, 2)
            pe.wait_ge(edge_halves, 3)
            for a, halves in enumerate(((within_half,), (key_high, key_low))):
                for at in range(0, NSTEPS, 512):
                    n = min(512, NSTEPS - at)
                    ops = [(half[:, g, :], chosen[g][:, at:at + n]) for half in halves for g in range(EG)]
                    for i, (half, picks) in enumerate(ops):
                        last = m((agg_ps, window_ps)[a][:, at // 512, 0:n], half, picks, start=(i == 0),
                                 stop=(i == len(ops) - 1))
                last.then_inc(steps_turned, 1)
            h0_turn(0)
            pe.wait_ge(ranges_found, 2)
            pe.wait_ge(lo_copied, 1)
            turn_range(hi)
            pe.wait_ge(consts_made, CONSTS)

            def squares(i):
                sq, width, halves = ((wsq1, D, 2), (wsq2, F2, 2), (wsq3, D, 1))[i]
                pe.wait_ge(squares_made, 2)
                if i == 0:
                    pe.wait_ge(h0T_copied, 2 * NCH)
                if i == 2:
                    pe.wait_ge(norms_made, 1)
                for j in range(2):
                    for k in range(halves):
                        last = m(lin_ps[:, i % 2, j * width:(j + 1) * width], ones32,
                                 sq[j][:, k, :] if halves == 2 else sq[j], start=(k == 0), stop=(k == halves - 1))
                last.then_inc(squares_summed, 1)

            def open_window(bank):
                m(window_ps[:, bank, 2 * KEYS:2 * KEYS + 2], ones16[:, :], ones16[:, 0:2], start=True, stop=False)

            def close_window(bank, done):
                m(window_ps[:, bank, 2 * KEYS:2 * KEYS + 2], ones16[:, :], ones16[:, 0:2], start=False,
                  stop=True).then_inc(done, 1)

            def step(w, i):
                at, k = FILL_AT[w], HOT_AT[w] + i
                if i == 0:
                    if at >= 2:
                        pe.wait_ge(window_stored, at - 1)
                    open_window(at % 2)
                cols = slice(0, KEYS) if i < STEPS[2 * w] else slice(KEYS, 2 * KEYS)
                if k % RING == 0:
                    pe.wait_ge(hot_made, k // RING + 1)
                m(window_ps[:, at % 2, cols], hot_src[:, k // RING % GROUPS, :, k % RING],
                  hot_key[:, k // RING % GROUPS, :, k % RING], start=False, stop=False).then_inc(hot_used, 1)
                if i == steps_of([w]) - 1:
                    close_window(at % 2, window_counted)

            regs = heavy_registers(pe, "pe")
            batches = pe.alloc_register("pe_batches")
            done_heavy = pe.alloc_register("pe_heavy")
            pe.reg_mov(batches, 0)
            pe.reg_mov(done_heavy, 0)
            pe.sem_inc(batch_used, 1)
            pe.sem_inc(heavy_stored, 1)

            def heavy_of(q):
                if not DUE.get(q):
                    return
                pe.wait_ge(window_stored, filled_after(q))

                def add(w, first, n):
                    pe.wait_ge(heavy_stored, pe.snap(done_heavy, min_val=0, max_val=NWIN) + 1)
                    open_window(0)
                    m(window_ps[:, 0, 0:KEYS].rearrange("p (w t) -> p t w", w=WIN), ident16[:, :],
                      counts[:, :, bass.ds(w * WIN, WIN)], start=False, stop=False)
                    with pe.Fori(0, n):
                        pe.wait_ge(batch_made, pe.snap(batches, min_val=0, max_val=NWIN * ET) + 1)
                        for j in range(BATCH):
                            last = m(window_ps[:, 0, 0:KEYS], hot_src[:, heavy_group(q), :, j],
                                     hot_key[:, heavy_group(q), :, j], start=False, stop=False)
                        last.then_inc(batch_used, 1)
                        pe.reg_add(batches, batches, 1)
                    close_window(0, heavy_counted)
                    pe.reg_add(done_heavy, done_heavy, 1)

                for c in DUE[q]:
                    heavy_windows(pe, c, regs, add)
                pe.wait_ge(heavy_stored, pe.snap(done_heavy, min_val=0, max_val=NWIN) + 1)

            def lin(l, q):
                n, t = size_of(chunk_at(q))
                pe.wait_ge(agg_scaled[l], AGG[l] * (q + 1))
                pe.wait_ge(self_loaded[l], 16 * (q + 1))
                if l == 2 and isinstance(q, int) and q == 0:
                    pe.wait_ge(late_loaded, LATE)
                if l == 4:
                    if not isinstance(q, int) or q > 0:
                        pe.wait_ge(out_made, both(q, 2, 1))
                    for g in range(2 if n == CH else 1):
                        for i in range(2 if n == CH else 1):
                            rows_ = P if n == CH else n
                            node = (2 * g + i) * P
                            ops = [(aggT[:, k, node:node + rows_], W14[:, 0, k, :]) for k in range(2)]
                            ops += [(selfT[:, k, node:node + rows_], W14[:, 1, k, :]) for k in range(2)]
                            for j, (h, w) in enumerate(ops):
                                last = m(lin_ps[0:rows_, g, i * D:(i + 1) * D], h, w, start=(j == 0),
                                         stop=(j == len(ops) - 1))
                        last.then_inc(lin_done[4], 1)
                    return
                if l > 1 and (not isinstance(q, int) or q > 0):
                    pe.wait_ge(relu_done[l], NEW[l] * q)
                for h in range(1 if l == 2 else 2):
                    cols = slice(h * P, (h + 1) * P)
                    if l == 1:
                        ops = [(W14[:, 0, k, cols], aggT[:, k, 0:n]) for k in range(2)]
                        ops += [(W14[:, 1, k, cols], selfT[:, k, 0:n]) for k in range(2)]
                    elif l == 2:
                        ops = [(Wr2_sb[:, k, :], selfT[:, k, 0:n]) for k in range(2)]
                    else:
                        ops = [(W3[:, 0, cols], aggT[:, 0, 0:n]), (W3[:, 1, cols], selfT[:, 0, 0:n])]
                    for i, (w, r) in enumerate(ops):
                        last = m(lin_ps[:, h, 0:n], w, r, start=(i == 0), stop=(i == len(ops) - 1))
                    last.then_inc(lin_done[l], 1)

            def narrow(q):
                n, t = size_of(chunk_at(q))
                pe.wait_ge(relu_done[1], 2 * (q + 1))
                for k in range(2):
                    last = m(lin_ps[:, 0, 0:n], Wl2_sb[:, k, :], newT[:, k, 0:n], start=(k == 0), stop=(k == 1))
                last.then_inc(narrow_done, 1)

            def turn(l, q, h):
                n, t = size_of(chunk_at(q))
                pe.wait_ge(low_done[l], TURNS[l] * q + h + 1)
                if not (isinstance(q, int) and q == 0 and h == 0):
                    pe.wait_ge(turn_copied[l], TURNS[l] * q + h)
                rows_ = P if n == CH else n
                for i in range(t):
                    for part in range(2):
                        last = nc.tensor.transpose(turn_ps[0:rows_, 2 * i + part, :],
                                                   partsT[:, part, i * P:i * P + rows_], ident16[:, :])
                last.then_inc(turned[l], 1)

            def add_sources(l, q, bank, k, first, final, halves=None):
                c = chunk_at(q)
                n, t = size_of(c)
                H_of = H if AGG[l] == 2 else Hn
                for h in halves or range(AGG[l]):
                    for part in range(2):
                        last = m((agg_ps, window_ps)[bank][:, h, 0:n], H_of[:, k, part, h * P:(h + 1) * P],
                                 counts[:, k, chunk_cols(c, n)], start=first and part == 0,
                                 stop=final and part == 1)
                    if final:
                        last.then_inc(agg_done[l], 1)

            def add_degrees(q):
                c = chunk_at(q)
                n, t = size_of(c)
                rows_ = P if n == CH else n
                if q == 0:
                    pe.wait_ge(h0T_copied, 2 * NCH)
                elif q == 1:
                    pe.wait_ge(norms_made, 3)
                else:
                    pe.wait_ge(low_done[1], q - 1)
                for i in range(t):
                    for k in range(NT):
                        last = m(lin_ps[0:rows_, 0, 2 * i:2 * i + 2], counts[:, k, bass.ds((c * TPC + i) * P, rows_)],
                                 ones16[:, 0:2], start=(k == 0), stop=(k == NT - 1))
                last.then_inc(degree_done, 1)

            def turn_degrees(q):
                n, t = size_of(chunk_at(q))
                rows_ = P if n == CH else n
                pe.wait_ge(degree_inverted, q + 1)
                if q >= 1:
                    pe.wait_ge(rdeg_made, q)
                for i in range(t):
                    last = m(degree_ps[:, i * P:i * P + rows_],
                             rdeg_columns[0:rows_, q, i:i + 1].broadcast_to([rows_, P]), ident32[0:rows_, 0:rows_], start=True, stop=True)
                last.then_inc(degree_turned, 1)

            pe.wait_ge(step_tables, 2 * -(-NSTEPS // 512))
            for i, w in enumerate(FILLS[-1]):
                if i % SLOTS == 0 and i // SLOTS + 1 < NCH:
                    h0_turn(i // SLOTS + 1)
                for j in range(steps_of([w])):
                    step(w, j)
            load_heavy(pe, regs)
            heavy_of(-1)
            pe.wait_ge(h0_low, NCH)
            for q in range(NCH):
                pe.wait_ge(window_stored, filled_after(q - 1))
                add_degrees(q)
                if q >= 1:
                    pe.wait_ge(agg_scaled[1], 2 * q)
                for kind, k in script(q):
                    if kind == "step":
                        step(*k)
                    if kind == "half":
                        add_sources(1, q, 0, k, k == 0, k == NT - 1, halves=(1,))
                    if kind != "sum":
                        continue
                    if k == 1:
                        pe.wait_ge(degree_inverted, q + 1)
                    add_sources(1, q, 0, k, k == 0, k == NT - 1, halves=(0,))
                    if q == 0 and k in (2, 3, 7):
                        squares((2, 3, 7).index(k))
                    if k == DEGREE_TURN_K:
                        turn_degrees(q)
                    if q >= 1 and k == LIN_K:
                        lin(1, q - 1)
                    if q >= 1 and k == NARROW_K:
                        narrow(q - 1)
                    if q >= 1 and k == TURN_K:
                        turn(1, q - 1, 0)
                heavy_of(q)
            def rest(l, q):
                return {1: {1: [lambda: lin(1, q)], 8: [lambda: narrow(q)], 14: [lambda: turn(1, q, 0)]},
                        2: {6: [lambda: lin(2, q)], 18: [lambda: turn(2, q, 0)]},
                        3: {6: [lambda: lin(3, q)], 16: [lambda: turn(3, q, 0)], 22: [lambda: turn(3, q, 1)]},
                        4: {4: [lambda: lin(4, q)]}}[l]


            for l in (2, 3, 4):
                def place(q, bank):
                    between = rest(l, q - 1)
                    if not isinstance(q, int) or q > 1:
                        pe.wait_ge(agg_scaled[l], AGG[l] * (q - 1))
                    for k in range(NT):
                        add_sources(l, q, bank, k, k == 0, k == NT - 1)
                        for do in between.get(k, []):
                            do()

                pe.wait_ge(agg_scaled[l - 1], AGG[l - 1] * NCH)
                tiles = [(c, k) for c in ORDER for k in range(c * TPC, min((c + 1) * TPC, NT))]
                left = [do for _, dos in sorted(rest(l - 1, NCH - 1).items()) for do in dos]
                for i, (c, k) in enumerate(tiles):
                    if i in REST_AT[l - 1]:
                        left.pop(0)()
                    pe.wait_ge(H_loaded[c], 16 * (l - 1))
                    add_sources(l, 0, 0, k, i == 0, i == NT - 1)
                over_places(pe, place)
            lin(4, NCH - 1)



_INS = ['x', 'src', 'dst'] + [f'L0_gnn_{w}{i}' for i in (1, 2, 3, 4) for w in ('Wl', 'Wr', 'b')]


def kernel(**inputs):
    import numpy as _np
    import concourse.bacc as _bacc
    from concourse import mybir as _mybir
    from concourse.bass_utils import run_bass_kernel_spmd as _run

    nc = _bacc.Bacc("TRN2", target_bir_lowering=False, num_devices=1, dynamic_dma_scratch_size=1024)
    arrays, args = {}, []
    for name in _INS:
        a = _np.ascontiguousarray(inputs[name])
        arrays[f"in_{name}_dram"] = a
        args.append(nc.dram_tensor(f"in_{name}_dram", a.shape, _mybir.dt.from_np(a.dtype), kind="ExternalInput").ap())
    args.append(nc.dram_tensor("out_0_dram", inputs['x'].shape, _mybir.dt.float32, kind="ExternalOutput").ap())
    sage_stack_kernel(nc, *args)
    r = _run(nc, [arrays], core_ids=[0])
    return r.results[0]["out_0_dram"]
```
